# Optimizing a Trainium2 kernel written in Bass

```python
import numpy as np
import jax
import jax.numpy as jnp

def _softmax(x, axis=-1):
    return jax.nn.softmax(x, axis=axis)

def _gelu(x):
    return jax.nn.gelu(x, approximate=True)

def _silu(x):
    return jax.nn.silu(x)

def _sigmoid(x):
    return jax.nn.sigmoid(x)

def _layernorm(x, axis=-1, eps=1e-05):
    m = jnp.mean(x, axis=axis, keepdims=True)
    v = jnp.var(x, axis=axis, keepdims=True)
    return (x - m) / jnp.sqrt(v + eps)

def _scatter_add(tgt, idx, src, axis=0):
    return tgt.at[idx].add(src)

def _segment_sum(src, seg, n):
    return jax.ops.segment_sum(src, seg, n)
kernel_name = 'mk_metaformer_d1_conv_nchw256_r2_adef15'

def setup_inputs(seed: int=0):
    np.random.seed(seed)
    _w = jnp.asarray

    def _rec_inputs():
        import jax
        import jax.numpy as jnp
        _gk = jax.random.key(seed)
        x = -0.0003929 + 0.9999 * jax.random.normal(jax.random.fold_in(_gk, 1), (16, 128, 32, 32), jnp.float32)
        return x
    x = _rec_inputs()

    def _L0_conv_setup():
        import jax, jax.numpy as jnp
        import numpy as np
        HEADS = 4
        HEAD_DIM = 32
        DIM = 128
        HIDDEN = HEADS * HEAD_DIM
        SCALE = HEAD_DIM ** (-0.5)

        def rmsnorm(x, g):
            inv = jax.lax.rsqrt(jnp.sum(x * x, axis=1, keepdims=True) + 1e-12)
            return x * inv * (g * x.shape[1] ** 0.5)[None, :, None, None]
        key = jax.random.key(seed)
        k1, k2, k3 = jax.random.split(key, 3)
        b, H, W = (16, 32, 32)
        x = jax.random.normal(k1, (b, DIM, H, W), dtype=jnp.float32)
        W_qkv = jax.random.normal(k2, (3 * HIDDEN, DIM), dtype=jnp.float32) * DIM ** (-0.5)
        W_out = jax.random.normal(k3, (DIM, HIDDEN), dtype=jnp.float32) * HIDDEN ** (-0.5)
        b_out = jnp.zeros((DIM,), dtype=jnp.float32)
        g_norm = jnp.ones((DIM,), dtype=jnp.float32)
        g_out = jnp.ones((DIM,), dtype=jnp.float32)
        return {'x': x, 'W_qkv': W_qkv, 'W_out': W_out, 'b_out': b_out, 'g_norm': g_norm, 'g_out': g_out}
    _L0_conv_all = _L0_conv_setup()
    _L0_conv_in = {k: v for k, v in _L0_conv_all.items() if k in ('W_qkv', 'W_out', 'b_out', 'g_norm', 'g_out')}
    del _L0_conv_all

    def _L0_ffn_setup():
        import jax, jax.numpy as jnp
        import numpy as np
        B, T, D, H, E = (16, 2048, 128, 256, 8)
        key = jax.random.key(seed)
        ks = jax.random.split(key, 5)
        x = jax.random.normal(ks[0], (B, T, D), dtype=jnp.float32)
        gate_w = jax.random.normal(ks[1], (D, E), dtype=jnp.float32) * 0.02
        gate_b = jnp.zeros((E,), dtype=jnp.float32)
        W1 = jax.random.normal(ks[2], (E, D, H), dtype=jnp.float32) * 0.02
        b1 = jnp.zeros((E, H), dtype=jnp.float32)
        W2 = jax.random.normal(ks[3], (E, H, D), dtype=jnp.float32) * 0.02
        b2 = jnp.zeros((E, D), dtype=jnp.float32)
        return {'x': x, 'gate_w': gate_w, 'gate_b': gate_b, 'W1': W1, 'b1': b1, 'W2': W2, 'b2': b2}
    _L0_ffn_all = _L0_ffn_setup()
    _L0_ffn_in = {k: v for k, v in _L0_ffn_all.items() if k in ('gate_w', 'gate_b', 'W1', 'b1', 'W2', 'b2')}
    del _L0_ffn_all
    return {'x': x, 'L0_conv_W_qkv': _L0_conv_in['W_qkv'], 'L0_conv_W_out': _L0_conv_in['W_out'], 'L0_conv_b_out': _L0_conv_in['b_out'], 'L0_conv_g_norm': _L0_conv_in['g_norm'], 'L0_conv_g_out': _L0_conv_in['g_out'], 'L0_ffn_gate_w': _L0_ffn_in['gate_w'], 'L0_ffn_gate_b': _L0_ffn_in['gate_b'], 'L0_ffn_W1': _L0_ffn_in['W1'], 'L0_ffn_b1': _L0_ffn_in['b1'], 'L0_ffn_W2': _L0_ffn_in['W2'], 'L0_ffn_b2': _L0_ffn_in['b2']}

def reference(x, L0_conv_W_qkv, L0_conv_W_out, L0_conv_b_out, L0_conv_g_norm, L0_conv_g_out, L0_ffn_gate_w, L0_ffn_gate_b, L0_ffn_W1, L0_ffn_b1, L0_ffn_W2, L0_ffn_b2):
    import jax
    import jax.numpy as jnp

    def _L0_conv_ref(x, W_qkv, W_out, b_out, g_norm, g_out):
        import jax, jax.numpy as jnp
        import numpy as np
        HEADS = 4
        HEAD_DIM = 32
        DIM = 128
        HIDDEN = HEADS * HEAD_DIM
        SCALE = HEAD_DIM ** (-0.5)

        def rmsnorm(x, g):
            inv = jax.lax.rsqrt(jnp.sum(x * x, axis=1, keepdims=True) + 1e-12)
            return x * inv * (g * x.shape[1] ** 0.5)[None, :, None, None]
        b, c, H, W = x.shape
        n = H * W
        xn = rmsnorm(x, g_norm)
        qkv = jnp.einsum('bchw,oc->bohw', xn, W_qkv)
        qkv = qkv.reshape(b, 3, HEADS, HEAD_DIM, n)
        q, k, v = (qkv[:, 0], qkv[:, 1], qkv[:, 2])
        q = jax.nn.softmax(q, axis=-2)
        k = jax.nn.softmax(k, axis=-1)
        context = jnp.einsum('bhdn,bhen->bhde', k, v)
        out = jnp.einsum('bhde,bhdn->bhen', context, q) * SCALE
        out = out.reshape(b, HIDDEN, H, W)
        out = jnp.einsum('bchw,oc->bohw', out, W_out) + b_out[None, :, None, None]
        return rmsnorm(out, g_out)

    def _L0_ffn_ref(x, gate_w, gate_b, W1, b1, W2, b2):
        import jax, jax.numpy as jnp
        import numpy as np
        B, T, D, H, E = (16, 2048, 128, 256, 8)
        Bb, Tt, Dd = x.shape
        Ee = gate_w.shape[1]
        xf = x.reshape(-1, Dd)
        N = xf.shape[0]
        logits = xf @ gate_w + gate_b
        probs = jax.nn.softmax(logits, axis=-1)
        top2_vals, top2_idx = jax.lax.top_k(probs, 2)
        cw = jnp.zeros((N, Ee), dtype=xf.dtype).at[jnp.arange(N)[:, None], top2_idx].add(top2_vals)

        def step(acc, params):
            w1, bb1, w2, bb2, we = params
            h = jax.nn.gelu(xf @ w1 + bb1, approximate=False)
            y = h @ w2 + bb2
            return (acc + we[:, None] * y, None)
        out, _ = jax.lax.scan(step, jnp.zeros_like(xf), (W1, b1, W2, b2, cw.T))
        return out.reshape(Bb, Tt, Dd)

    def _gn(v, G=32, eps=1e-05):
        B_, C_, H_, W_ = v.shape
        g = v.reshape(B_, G, C_ // G, H_, W_)
        m = jnp.mean(g, axis=(2, 3, 4), keepdims=True)
        s = jnp.var(g, axis=(2, 3, 4), keepdims=True)
        return ((g - m) / jnp.sqrt(s + eps)).reshape(v.shape)

    def _ln_c(v, eps=1e-06):
        m = jnp.mean(v, axis=1, keepdims=True)
        s = jnp.var(v, axis=1, keepdims=True)
        return (v - m) / jnp.sqrt(s + eps)

    def _ln_t(v, eps=1e-05):
        m = jnp.mean(v, axis=-1, keepdims=True)
        s = jnp.var(v, axis=-1, keepdims=True)
        return (v - m) / jnp.sqrt(s + eps)

    def _to_tokens(v):
        B_, C_, H_, W_ = v.shape
        return v.reshape(B_, C_, H_ * W_).transpose(0, 2, 1)

    def _from_tokens(t, like):
        B_, C_, H_, W_ = like.shape
        return t.transpose(0, 2, 1).reshape(B_, C_, H_, W_)
    x = x + _L0_conv_ref(_ln_c(x), L0_conv_W_qkv, L0_conv_W_out, L0_conv_b_out, L0_conv_g_norm, L0_conv_g_out)
    t = _to_tokens(x)
    t = t + _L0_ffn_ref(_ln_t(t), L0_ffn_gate_w, L0_ffn_gate_b, L0_ffn_W1, L0_ffn_b1, L0_ffn_W2, L0_ffn_b2)
    x = _from_tokens(t, x)
    return x

_drawn_inputs = setup_inputs


def setup_inputs(seed=0):
    import zlib

    import numpy as np

    out = dict(_drawn_inputs(seed))
    spreads = {'L0_conv_b_out': (0.0, 0.1),
     'L0_conv_g_norm': (1.0, 0.6),
     'L0_conv_g_out': (1.0, 0.2),
     'L0_ffn_gate_b': (0.0, 0.616),
     'L0_ffn_b1': (0.0, 0.8),
     'L0_ffn_b2': (0.0, 0.515)}
    factors = {'L0_ffn_gate_w': 4.05, 'L0_ffn_W1': 8.0, 'L0_ffn_W2': 8.0}
    for name, (base, spread) in spreads.items():
        noise = np.random.default_rng([zlib.crc32(name.encode()), seed]).standard_normal(out[name].shape)
        drawn = base * np.exp(spread * noise) if base else spread * noise
        out[name] = jnp.asarray(drawn.astype(out[name].dtype))
    for name, factor in factors.items():
        out[name] = (out[name] * factor).astype(out[name].dtype)
    return out
```

```python
from contextlib import ExitStack

import concourse.bass as bass
from concourse import mybir

ALU = mybir.AluOpType
ACT = mybir.ActivationFunctionType
X_AXIS = mybir.AxisListType.X
F32 = mybir.dt.float32
F32R = mybir.dt.float32r

P = 128
BATCH, CH, TOK = 16, 128, 1024
TILES = TOK // P
HALF = TOK // 2
HT = HALF // P
HEADS, HEAD_DIM = 4, 32
EXPERTS, HIDDEN = 8, 256
KT = HIDDEN // P
SLOTS = 2 * EXPERTS * KT
UNITS = 2 * EXPERTS
AHEAD = 3
HB = 4
LN_C_EPS, LN_T_EPS, RMS_EPS = 1e-6, 1e-5, 1e-12

BANK_USES = [("F0", 0, 2), ("F1", 1, 2), ("X0", 0, 1), ("X1", 1, 1), ("O0", 0, 2), ("O1", 1, 2),
             ("G0", 0, 2), ("G1", 1, 2), ("Q0", 0, 1), ("Q1", 1, 1), ("Q2", 0, 1), ("Q3", 1, 1),
             ("Q4", 0, 1), ("Q5", 1, 1), ("Q6", 0, 1), ("Q7", 1, 1), ("L", 0, 2), ("KT", 1, 1),
             ("KB", 0, 1), ("CW", 1, 2), ("C", 0, 1), ("T0", 1, 1), ("M", 0, 1), ("T1", 1, 1)]
BANK_OF = {name: bank for name, bank, _ in BANK_USES}


class Image:

    def __init__(self, pair, parity):
        self.pair, self.parity = pair, parity
        self.index = pair * 2 + parity

    def plus(self, n):
        return Image(self.pair + (self.parity + n) // 2, (self.parity + n) % 2)


def wait(eng, sem, value):
    if not isinstance(value, int) or value > 0:
        eng.wait_ge(sem, value)


def build(nc, x, w_qkv, w_out, b_out, g_norm, g_out, gate_w, gate_b, w1, b1, w2, b2, out):
    x_dram = x.rearrange("b c h w -> (b c) (h w)")
    out_dram = out.rearrange("b c h w -> (b c) (h w)")
    w1_dram = w1.rearrange("e c h -> c e h")
    w2_dram = w2.rearrange("e (k p) d -> p (e k) d", p=P)
    scratch = nc.dram_tensor("routing_scratch", [2 * EXPERTS * TILES, P], F32, kind="Internal").ap()

    with ExitStack() as ctx:
        def sb(name, shape, dt=F32):
            return ctx.enter_context(nc.sbuf_tensor(name, shape, dt))

        def sem(name):
            return ctx.enter_context(nc.semaphore(name))

        hidden_ps = ctx.enter_context(nc.psum_tensor("hidden_ps", [P, HB, HALF], F32))
        y_ps = ctx.enter_context(nc.psum_tensor("y_ps", [P, 2, HALF], F32))
        ab = ctx.enter_context(nc.psum_tensor("ab", [P, 2, HALF], F32))

        ident = sb("ident", [P, P])
        ones = sb("ones", [P, P])
        head_mask = sb("head_mask", [P, P])
        minus_half = sb("minus_half", [P, TILES])
        rms_eps = sb("rms_eps", [P, TILES])
        turn_in, turn_out = sb("turn_in", [P, 1]), sb("turn_out", [P, 1])
        rank = sb("rank", [P, EXPERTS])
        g_norm_bc = sb("g_norm_bc", [P, P])
        g_out_bc = sb("g_out_bc", [P, P])
        b_out_bc = sb("b_out_bc", [P, P])
        gate_b_bc = sb("gate_b_bc", [P, EXPERTS])
        gate_w_sb = sb("gate_w_sb", [P, EXPERTS])
        w_mean = sb("w_mean", [P, 3])
        w_out_raw = sb("w_out_raw", [P, P])
        b1_raw = sb("b1_raw", [EXPERTS * KT, P])
        b2_raw = sb("b2_raw", [EXPERTS, P])
        wqkv_h = sb("wqkv_h", [P, 3 * P], F32R)
        wqkv_l = sb("wqkv_l", [P, 3 * P], F32R)
        w_out_t = sb("w_out_t", [P, P])
        b1_t = sb("b1_t", [P, EXPERTS * KT])
        b2_t = sb("b2_t", [P, EXPERTS])
        w1h = sb("w1h", [P, EXPERTS, HIDDEN], F32R)
        w1l = sb("w1l", [P, EXPERTS, HIDDEN], F32R)
        w2h = sb("w2h", [P, EXPERTS * KT, CH], F32R)
        w2l = sb("w2l", [P, EXPERTS * KT, CH], F32R)

        x_sb = sb("x_sb", [P, 2, TOK])
        xh = sb("xh", [P, TOK], F32R)
        xl = sb("xl", [P, TOK], F32R)
        x_tok = sb("x_tok", [P, 2, TILES, CH])
        bn1 = sb("bn1", [P, TILES, 6])
        st1 = sb("st1", [P, 5, TILES])
        r1 = sb("r1", [P, TILES])
        qkv = sb("qkv", [P, TILES, 3 * P])
        q_stat = sb("q_stat", [P, 3, TILES * HEADS])
        k_part = sb("k_part", [P, P])
        k_max = sb("k_max", [P, 1])
        k_diag = sb("k_diag", [P, P])
        ctx_t = sb("ctx_t", [P, P])
        k_recip = sb("k_recip", [P, 1])
        mix = sb("mix", [P, 2, P])
        q_ch = sb("q_ch", [P, 2, TOK])

        square = sb("square", [P, 2, HALF])
        ss = sb("ss", [P, 2, TILES])
        r_rms = sb("r_rms", [P, TILES])
        x1_tok = sb("x1_tok", [P, TILES, CH])
        bn2 = sb("bn2", [P, TILES, 6])
        st2 = sb("st2", [P, 6, TILES])
        r2 = sb("r2", [P, TILES])
        xf_tok = sb("xf_tok", [P, TILES, CH])
        x1_ch = sb("x1_ch", [P, 2, TOK])
        xf_ch = sb("xf_ch", [P, TOK])
        xfh = sb("xfh", [P, 2, TOK], F32R)
        xfl = sb("xfl", [P, 2, TOK], F32R)
        gate = sb("gate", [P, 6, TILES, EXPERTS])
        gate_stat = sb("gate_stat", [P, 7, TILES])
        cw_tok = sb("cw_tok", [P, 2, EXPERTS, TILES])
        cw_rows = sb("cw_rows", [EXPERTS * TILES, P])
        cw = sb("cw", [P, 2, EXPERTS, HALF])

        gh = sb("gh", [P, HB, HALF], F32R)
        gl = sb("gl", [P, HB, HALF], F32R)
        weighted = sb("weighted", [P, 2, HALF])

        wqkv_raw = cw[:, 0, 0, 0:3 * P].rearrange("p (j c) -> p j c", j=3)
        wqkv_c = cw[:, 0, 1, 0:3 * P].rearrange("p (j c) -> p j c", j=3)
        w1_raw = cw[:, 1, 0:4, :].rearrange("p a n -> p (a n)")
        w2_raw = cw[:, 1, 4:8, :].rearrange("p a n -> p (a n)")

        s_load_qkv, s_load_small, s_load_experts = sem("load_qkv"), sem("load_small"), sem("load_experts")
        s_const, s_ident = sem("const_done"), sem("ident_done")
        s_wqkv, s_wtr, s_wready = sem("wqkv_centered"), sem("weights_transposed"), sem("weights_ready")
        s_wsplit = sem("expert_weights_split")
        s_x_in = [sem("x_in0"), sem("x_in1")]
        s_x_split = sem("x_split")
        s_x_tr = sem("x_transposed")
        s_x_tok = sem("x_tok_done")
        s_st1 = sem("stats1_step")
        s_r1 = sem("r1_done")
        s_qkv_mm, s_qkv = sem("qkv_product"), sem("qkv_scaled")
        s_q_max, s_k_part = sem("q_max"), sem("k_part_max")
        s_q_sub, s_k_sub = sem("q_shifted"), sem("k_shifted")
        s_kt_mm, s_k_max, s_kb_mm = sem("k_max_transposed"), sem("k_max_step"), sem("k_max_spread")
        s_exp = sem("exp_done")
        s_q_sum, s_q_norm = sem("q_sum_step"), sem("q_normalised")
        s_c_mm, s_ctx, s_m_mm, s_mix = sem("context"), sem("context_step"), sem("mix_product"), sem("mix_done")
        s_q_tr, s_q_ch = sem("q_transposed"), sem("q_ch_done")
        s_fin, s_square, s_ss = sem("attention_out"), sem("square_done"), sem("square_sum")
        s_rms, s_y, s_x1 = sem("rms_step"), sem("normed_out"), sem("x1_done")
        s_st2, s_r2, s_xf = sem("stats2_step"), sem("r2_done"), sem("xf_done")
        s_o_tr, s_x1_ch = sem("x1_transposed"), sem("x1_ch_done")
        s_g_tr, s_xf_ch = sem("xf_transposed"), sem("xf_ch_done")
        s_xf_split = sem("xf_split")
        s_lg_mm, s_gate, s_gate_exp = sem("logits"), sem("gate_step"), sem("gate_exp")
        s_cw_mm, s_cw_rows, s_scratch = sem("cw_transposed"), sem("cw_rows_done"), sem("cw_in_dram")
        s_cw_in = [[sem(f"cw_in{h}{q}") for q in range(2)] for h in range(2)]
        s_up, s_gelu, s_hi, s_lo = sem("up_done"), sem("gelu_done"), sem("high_done"), sem("low_done")
        s_down, s_weighted, s_added = sem("down_done"), sem("weighted_done"), sem("added_done")
        s_out = [[sem(f"stored{p}{h}") for h in range(2)] for p in range(2)]

        ST1, ST2, GATE = 5, 7, 19
        WREADY = 7
        POOL_CONSTS = 4 + EXPERTS
        CREDIT, STORE_CREDIT = 2, 16

        READ_OUT = {"F0": (s_y, 2, 1), "F1": (s_y, 2, 2), "X0": (s_x_tok, 2, 1), "X1": (s_x_tok, 2, 2),
                    "O0": (s_x1_ch, 2, 1), "O1": (s_x1_ch, 2, 2), "G0": (s_xf_ch, 2, 1), "G1": (s_xf_ch, 2, 2),
                    "L": (s_gate, GATE, 1), "KT": (s_k_max, 2, 1), "KB": (s_k_sub, 1, 1), "CW": (s_cw_rows, 1, 1),
                    "C": (s_ctx, 2, 2), "T0": (s_q_ch, 2, 1), "M": (s_mix, 1, 1), "T1": (s_q_ch, 2, 2)}
        READ_OUT.update({f"Q{t}": (s_qkv, TILES, t + 1) for t in range(TILES)})

        def last_read_of(name, a1, a2):
            order = [n for n, bank, _ in BANK_USES if bank == BANK_OF[name]]
            stage = {n: st for n, _, st in BANK_USES}
            image = {1: a1, 2: a2}
            for n in reversed(order[:order.index(name)]):
                if image[stage[n]] is not None:
                    s, per, k = READ_OUT[n]
                    return s, image[stage[n]].index * per + k
            s, per, k = READ_OUT[order[-1]]
            before = (a1.index if a1 is not None else BATCH) - 1
            return s, before * per + k

        def run(eng, body):
            body(None, Image(0, 0), None)
            body(None, Image(0, 1), Image(0, 0))
            with eng.Fori(0, BATCH // 2 - 1) as pair:
                for parity in range(2):
                    b = Image(pair, parity)
                    body(b, b.plus(2), b.plus(1))
            body(Image(BATCH // 2 - 1, 0), None, Image(BATCH // 2 - 1, 1))
            body(Image(BATCH // 2 - 1, 1), None, None)

        block = ctx.enter_context(nc.Block())

        @block.sync
        def _(sp):
            def load_x(a):
                wait(sp, s_x_split, (a.index - 1) * 2)
                wait(sp, s_x_tr, (a.index - 1) * 2)
                sp.dma_start(x_sb[:, a.parity, :], x_dram[bass.ds(a.index * P, P), :]).then_inc(s_x_in[a.parity], 16)

            sp.dma_start(wqkv_raw, w_qkv.rearrange("(j o) c -> o j c", j=3)).then_inc(s_load_qkv, 16)
            sp.dma_start(g_norm_bc[:, :], g_norm.partition_broadcast(P)).then_inc(s_load_qkv, 16)
            load_x(Image(0, 0))
            sp.dma_start(w1_raw.rearrange("p (e h) -> p e h", e=EXPERTS), w1_dram).then_inc(s_load_experts, 16)
            sp.dma_start(w2_raw.rearrange("p (e d) -> p e d", d=CH), w2_dram).then_inc(s_load_experts, 16)

            def body(b, a1, a2):
                if a1 is not None and not (b is None and a2 is None):
                    load_x(a1)
                if b is not None:
                    store(b, 0)
                if a2 is not None:
                    rows = EXPERTS * TILES
                    wait(sp, s_cw_rows, a2.index + 1)
                    sp.dma_start(scratch[a2.parity * rows:(a2.parity + 1) * rows, :], cw_rows[:, :]).then_inc(s_scratch, 16)
                    sp.wait_ge(s_scratch, (a2.index + 1) * 16)
                    for h in range(2):
                        if b is not None:
                            sp.wait_ge(s_weighted, b.index * UNITS + (h + 1) * EXPERTS + CREDIT)
                        elif h == 1:
                            sp.wait_ge(s_wsplit, 4)
                        for q in range(2):
                            half_rows = scratch[a2.parity * rows:(a2.parity + 1) * rows, :].rearrange(
                                "(e t) n -> e t n", e=EXPERTS)[q * 4:q * 4 + 4, h * HT:(h + 1) * HT, :]
                            sp.dma_start(cw[:, h, q * 4:q * 4 + 4, :],
                                         half_rows.rearrange("e t n -> e (t n)").partition_broadcast(P)
                                         ).then_inc(s_cw_in[h][q], 16)
                if b is not None:
                    store(b, 1)

            def store(b, h):
                sp.wait_ge(s_added, b.index * UNITS + (h + 1) * EXPERTS + CREDIT)
                sp.dma_start(out_dram[bass.ds(b.index * P, P), h * HALF:(h + 1) * HALF],
                             x1_ch[:, b.parity, h * HALF:(h + 1) * HALF]).then_inc(s_out[b.parity][h], 16)

            run(sp, body)
            for p in range(2):
                for h in range(2):
                    sp.wait_ge(s_out[p][h], 16 * (BATCH // 2) + STORE_CREDIT)

        @block.gpsimd
        def _(pool):
            def turnstile():
                pool.tensor_tensor(turn_out[:, :], turn_in[:, :], turn_in[:, :], ALU.add)

            pool.memset(ident[:, :], 0.0).then_inc(s_ident, 1)
            pool.memset(ones[:, :], 1.0).then_inc(s_const, 1)
            pool.memset(minus_half[:, :], -0.5).then_inc(s_const, 1)
            pool.memset(rms_eps[:, :], RMS_EPS).then_inc(s_const, 1)
            pool.memset(turn_in[:, :], 0.0).then_inc(s_const, 1)
            pool.memset(weighted[:, 0, 0:1], 0.0).then_inc(s_added, CREDIT)
            for p in range(2):
                for h in range(2):
                    pool.memset(weighted[:, 1, 2 * p + h:2 * p + h + 1], 0.0).then_inc(s_out[p][h], STORE_CREDIT)
            for e in range(EXPERTS):
                pool.memset(rank[:, e:e + 1], float(EXPERTS - e)).then_inc(s_const, 1)
            pool.wait_ge(s_ident, 1)
            pool.affine_select(out=ident[:, :], in_=ident[:, :], compare_op=ALU.not_equal, fill=1.0,
                               base=0, pattern=[[-1, P]], channel_multiplier=1).then_inc(s_ident, 1)
            pool.wait_ge(s_const, POOL_CONSTS)

            def add(b, s):
                u = s // KT
                h = u // EXPERTS
                dst = x1_ch[:, b.parity, h * HALF:(h + 1) * HALF]
                if u % EXPERTS == 0:
                    pool.wait_ge(s_x1_ch, b.index * 2 + h + 1)
                else:
                    pool.wait_ge(s_added, b.index * UNITS + u + CREDIT)
                pool.wait_ge(s_weighted, b.index * UNITS + u + 1 + CREDIT)
                pool.tensor_tensor(dst, dst, weighted[:, u % 2, :], ALU.add).then_inc(s_added, 1)

            def body(b, a1, a2):
                for s in range(SLOTS):
                    if a2 is not None:
                        n = a2.index
                        if s == 3:
                            wait(pool, s_y, n * 2)
                            pool.wait_ge(s_ss, n * 2 + 2)
                            pool.tensor_tensor(ss[:, 1, :], ss[:, 0, :], rms_eps[:, :], ALU.add).then_inc(s_rms, 1)
                            pool.wait_ge(s_rms, n * 2 + 1)
                            pool.tensor_tensor(r_rms[:, :], ss[:, 1, :], minus_half[:, :], ALU.pow).then_inc(s_rms, 1)
                        if s == 7:
                            pool.wait_ge(s_y, n * 2 + 2)
                            pool.tensor_tensor(x1_tok[:, :, :], x_tok[:, a2.parity, :, :], x1_tok[:, :, :],
                                               ALU.add).then_inc(s_x1, 1)
                        if s == 10:
                            pool.wait_ge(s_st2, n * ST2 + ST2)
                            pool.tensor_tensor(r2[:, :], st2[:, 3, :], minus_half[:, :], ALU.pow).then_inc(s_r2, 1)
                        if s == 14:
                            pool.wait_ge(s_xf_ch, n * 2 + 2)
                            if b is not None:
                                pool.wait_ge(s_up, b.index * SLOTS + AHEAD)
                            turnstile()
                            pool.tensor_scalar(xfh[:, a2.parity, :], xf_ch[:, :], 1.0, None, ALU.mult).then_inc(s_xf_split, 1)
                        if s == 15:
                            pool.wait_ge(s_xf_split, n * 2 + 1)
                            pool.tensor_tensor(xfl[:, a2.parity, :], xf_ch[:, :],
                                               xfh[:, a2.parity, :].bitcast(F32), ALU.subtract).then_inc(s_xf_split, 1)
                    if a1 is not None:
                        n = a1.index
                        if s == 5:
                            pool.wait_ge(s_x_in[a1.parity], a1.pair * 16 + 16)
                            wait(pool, s_qkv_mm, n * TILES)
                            turnstile()
                            pool.tensor_scalar(xh[:, :], x_sb[:, a1.parity, :], 1.0, None, ALU.mult).then_inc(s_x_split, 1)
                        if s == 6:
                            pool.wait_ge(s_x_split, n * 2 + 1)
                            pool.tensor_tensor(xl[:, :], x_sb[:, a1.parity, :], xh[:, :].bitcast(F32),
                                               ALU.subtract).then_inc(s_x_split, 1)
                        if s == 12:
                            wait(pool, s_qkv, n * TILES)
                            pool.wait_ge(s_st1, n * ST1 + ST1)
                            pool.tensor_tensor(r1[:, :], st1[:, 4, :], minus_half[:, :], ALU.pow).then_inc(s_r1, 1)
                        if s == 20:
                            pool.wait_ge(s_q_max, n + 1)
                            q = qkv[:, :, 0:P].rearrange("p t (h d) -> p t h d", d=HEAD_DIM)
                            m = q_stat[:, 0, :].rearrange("p (t h) -> p t h", h=HEADS).unsqueeze(3).broadcast_to(
                                (P, TILES, HEADS, HEAD_DIM))
                            pool.tensor_tensor(q, q, m, ALU.subtract).then_inc(s_q_sub, 1)
                        if s == 25:
                            pool.wait_ge(s_q_sum, n * 2 + 2)
                            q = qkv[:, :, 0:P].rearrange("p t (h d) -> p t h d", d=HEAD_DIM)
                            m = q_stat[:, 2, :].rearrange("p (t h) -> p t h", h=HEADS).unsqueeze(3).broadcast_to(
                                (P, TILES, HEADS, HEAD_DIM))
                            pool.tensor_tensor(q, q, m, ALU.mult).then_inc(s_q_norm, 1)
                    if b is not None and s % KT == 1 and s > 1:
                        add(b, s - KT)
                if b is not None:
                    add(b, SLOTS - 1)

            run(pool, body)

        @block.scalar
        def _(act):
            act.dma_start(w_out_raw[:, :], w_out).then_inc(s_load_small, 16)
            act.dma_start(b1_raw[:, :], b1.rearrange("e (k p) -> (e k) p", p=P)).then_inc(s_load_small, 16)
            act.dma_start(b2_raw[:, :], b2).then_inc(s_load_small, 16)
            act.dma_start(g_out_bc[:, :], g_out.partition_broadcast(P)).then_inc(s_load_small, 16)
            act.dma_start(b_out_bc[:, :], b_out.partition_broadcast(P)).then_inc(s_load_small, 16)
            act.dma_start(gate_b_bc[:, :], gate_b.partition_broadcast(P)).then_inc(s_load_small, 16)
            act.dma_start(gate_w_sb[:, :], gate_w).then_inc(s_load_small, 16)

            def gelu(b, s):
                act.wait_ge(s_up, b.index * SLOTS + s + 1)
                bank = hidden_ps[:, s % HB, :]
                act.activation(bank, bank, ACT.Gelu, bias=b1_t[:, s % UNITS:s % UNITS + 1]).then_inc(s_gelu, 1)

            def high(b, s):
                act.wait_ge(s_gelu, b.index * SLOTS + s + 1)
                act.activation(gh[:, s % HB, :], hidden_ps[:, s % HB, :], ACT.Copy).then_inc(s_hi, 1)

            def body(b, a1, a2):
                for s in range(SLOTS):
                    if a2 is not None:
                        n = a2.index
                        if s in (1, 2):
                            h = s - 1
                            act.wait_ge(s_fin, n * 2 + h + 1)
                            act.activation(square[:, h, :], ab[:, h, :], ACT.Square).then_inc(s_square, 1)
                        if s in (10, 11):
                            h = s - 10
                            if h == 0:
                                for k in range(2):
                                    act.wait_ge(s_out[a2.parity][k], a2.pair * 16 + STORE_CREDIT)
                            act.wait_ge(s_o_tr, n * 2 + h + 1)
                            act.activation(x1_ch[:, a2.parity, h * HALF:(h + 1) * HALF], ab[:, h, :],
                                           ACT.Copy).then_inc(s_x1_ch, 1)
                        if s in (13, 14):
                            h = s - 13
                            act.wait_ge(s_g_tr, n * 2 + h + 1)
                            if h == 0:
                                wait(act, s_xf_split, n * 2)
                                wait(act, s_lg_mm, n)
                            act.activation(xf_ch[:, h * HALF:(h + 1) * HALF], ab[:, h, :], ACT.Copy).then_inc(s_xf_ch, 1)
                        if s == 23:
                            act.wait_ge(s_gate, n * GATE + 3)
                            act.activation(gate[:, 1, :, :], gate[:, 0, :, :], ACT.Exp).then_inc(s_gate_exp, 1)
                        if s == 26:
                            wait(act, s_scratch, n * 16)
                            act.wait_ge(s_cw_mm, n + 1)
                            act.activation(cw_rows[:, :], ab[0:EXPERTS * TILES, BANK_OF["CW"], 0:P],
                                           ACT.Copy).then_inc(s_cw_rows, 1)
                    if a1 is not None:
                        n = a1.index
                        if s in (8, 9):
                            h = s - 8
                            if h == 0:
                                wait(act, s_x1, n - 1)
                            act.wait_ge(s_x_tr, n * 2 + h + 1)
                            act.activation(x_tok[:, a1.parity, h * HT:(h + 1) * HT, :].rearrange("p t c -> p (t c)"),
                                           ab[:, h, :], ACT.Copy).then_inc(s_x_tok, 1)
                        if s == 23:
                            for sem_sub, j in ((s_q_sub, 0), (s_k_sub, 1)):
                                act.wait_ge(sem_sub, n + 1)
                                part = qkv[:, :, j * P:(j + 1) * P]
                                act.activation(part, part, ACT.Exp).then_inc(s_exp, 1)
                        if s in (28, 29):
                            h = s - 28
                            act.wait_ge(s_q_tr, n * 2 + h + 1)
                            if h == 0:
                                wait(act, s_fin, (n - 1) * 2)
                            act.activation(q_ch[:, a1.parity, h * HALF:(h + 1) * HALF], ab[:, BANK_OF[f"T{h}"], :],
                                           ACT.Copy).then_inc(s_q_ch, 1)
                    if b is not None:
                        if s + AHEAD < SLOTS:
                            gelu(b, s + AHEAD)
                        elif a2 is not None:
                            gelu(a2, s + AHEAD - SLOTS)
                        if s + AHEAD - 1 < SLOTS:
                            high(b, s + AHEAD - 1)
                        elif a2 is not None:
                            high(a2, s + AHEAD - 1 - SLOTS)
                if b is None and a2 is not None:
                    act.wait_ge(s_wready, WREADY)
                    gelu(a2, 0)
                    gelu(a2, 1)
                    high(a2, 0)
                    gelu(a2, 2)
                    high(a2, 1)

            run(act, body)

        @block.vector
        def _(dve):
            for i in range(HEADS):
                rows = slice(i * HEAD_DIM, (i + 1) * HEAD_DIM)
                for j in range(HEADS):
                    dve.memset(head_mask[rows, j * HEAD_DIM:(j + 1) * HEAD_DIM],
                               float(HEAD_DIM) ** -0.5 if i == j else 0.0)
            dve.memset(cw_tok[:, 1, :, :], 0.0)
            dve.memset(w_mean[:, 0:1], 0.0).then_inc(s_weighted, CREDIT)
            dve.wait_ge(s_weighted, CREDIT)
            dve.wait_ge(s_const, POOL_CONSTS)
            dve.wait_ge(s_ident, 2)
            dve.wait_ge(s_load_qkv, 32)
            dve.tensor_tensor(wqkv_c, wqkv_raw, g_norm_bc[:, :].unsqueeze(1).broadcast_to((P, 3, P)),
                              ALU.mult).then_inc(s_wqkv, 1)
            dve.wait_ge(s_wqkv, 1)
            dve.tensor_reduce(w_mean[:, :], wqkv_c, X_AXIS, ALU.add).then_inc(s_wqkv, 1)
            dve.wait_ge(s_wqkv, 2)
            dve.tensor_scalar(w_mean[:, :], w_mean[:, :], 1.0 / CH, None, ALU.mult).then_inc(s_wqkv, 1)
            dve.wait_ge(s_wqkv, 3)
            for j in range(3):
                dve.tensor_scalar(wqkv_raw[:, j, :], wqkv_c[:, j, :], w_mean[:, j:j + 1], None,
                                  ALU.subtract).then_inc(s_wqkv, 1)
            dve.wait_ge(s_load_small, 16 * 7)
            dve.tensor_scalar(g_out_bc[:, :], g_out_bc[:, :], float(CH) ** 0.5, None, ALU.mult).then_inc(s_wready, 1)
            dve.tensor_scalar(b_out_bc[:, :], b_out_bc[:, :], 1.0 / HEADS, None, ALU.mult).then_inc(s_wready, 1)
            dve.wait_ge(s_wtr, 1)
            dve.tensor_copy(wqkv_h[:, :], ab[:, 0, 0:3 * P]).then_inc(s_wready, 1)
            dve.wait_ge(s_wready, 3)
            dve.tensor_tensor(wqkv_l[:, :], ab[:, 0, 0:3 * P], wqkv_h[:, :].bitcast(F32), ALU.subtract).then_inc(s_wready, 1)
            dve.wait_ge(s_wtr, 2)
            dve.tensor_copy(w_out_t[:, :], ab[:, 1, 0:P]).then_inc(s_wready, 1)
            dve.tensor_copy(b1_t[:, :], ab[:, 1, P:P + EXPERTS * KT]).then_inc(s_wready, 1)
            dve.tensor_copy(b2_t[:, :], ab[:, 1, P + 16:P + 16 + EXPERTS]).then_inc(s_wready, 1)

            def split_experts():
                dve.wait_ge(s_load_experts, 32)
                w1f, w2f = (w[:, :, :].rearrange("p e n -> p (e n)") for w in (w1h, w2h))
                dve.tensor_copy(w1f, w1_raw).then_inc(s_wsplit, 1)
                dve.tensor_copy(w2f, w2_raw).then_inc(s_wsplit, 1)
                dve.wait_ge(s_wsplit, 2)
                dve.tensor_tensor(w1l[:, :, :].rearrange("p e n -> p (e n)"), w1_raw, w1f.bitcast(F32),
                                  ALU.subtract).then_inc(s_wsplit, 1)
                dve.tensor_tensor(w2l[:, :, :].rearrange("p e n -> p (e n)"), w2_raw, w2f.bitcast(F32),
                                  ALU.subtract).then_inc(s_wsplit, 1)

            def low(b, s):
                dve.wait_ge(s_hi, b.index * SLOTS + s + 1)
                dve.tensor_tensor(gl[:, s % HB, :], hidden_ps[:, s % HB, :], gh[:, s % HB, :].bitcast(F32),
                                  ALU.subtract).then_inc(s_lo, 1)

            def weigh(b, s):
                u = s // KT
                h, e = u // EXPERTS, u % EXPERTS
                if e % 4 == 0:
                    dve.wait_ge(s_cw_in[h][e // 4], b.index * 16 + 16)
                dve.wait_ge(s_added, b.index * UNITS + u - 1 + CREDIT)
                dve.wait_ge(s_down, b.index * UNITS + u + 1)
                dve.scalar_tensor_tensor(out=weighted[:, u % 2, :], in0=y_ps[:, u % 2, :], scalar=b2_t[:, e:e + 1],
                                         in1=cw[:, h, e, :], op0=ALU.add, op1=ALU.mult).then_inc(s_weighted, 1)

            def body(b, a1, a2):
                for s in range(SLOTS):
                    if a2 is not None:
                        n = a2.index
                        if s in (2, 3):
                            h = s - 2
                            if h == 0:
                                wait(dve, s_rms, n * 2)
                            dve.wait_ge(s_square, n * 2 + h + 1)
                            dve.tensor_reduce(ss[:, 0, h * HT:(h + 1) * HT],
                                              square[:, h, :].rearrange("p (t c) -> p t c", c=CH),
                                              X_AXIS, ALU.add).then_inc(s_ss, 1)
                        if s in (5, 6):
                            h = s - 5
                            dve.wait_ge(s_rms, n * 2 + 2)
                            if h == 0:
                                wait(dve, s_o_tr, n * 2)
                                wait(dve, s_xf, n)
                            for t in range(h * HT, (h + 1) * HT):
                                k = t - h * HT
                                last = dve.scalar_tensor_tensor(
                                    out=x1_tok[:, t, :], in0=ab[:, h, k * P:(k + 1) * P], scalar=r_rms[:, t:t + 1],
                                    in1=g_out_bc[:, :], op0=ALU.mult, op1=ALU.mult)
                            last.then_inc(s_y, 1)
                        if s in (8, 9):
                            h = s - 8
                            dve.wait_ge(s_x1, n + 1)
                            if h == 0:
                                wait(dve, s_r2, n)
                            for t in range(h * HT, (h + 1) * HT):
                                last = dve.bn_stats(bn2[:, t, :], x1_tok[:, t, :])
                        if s == 9:
                            base = n * ST2
                            last.then_inc(s_st2, 1)
                            dve.wait_ge(s_st2, base + 1)
                            stats2(base)
                        if s == 11:
                            dve.wait_ge(s_r2, n + 1)
                            wait(dve, s_g_tr, n * 2)
                            for t in range(TILES):
                                last = dve.tensor_scalar(xf_tok[:, t, :], x1_tok[:, t, :], st2[:, 5, t:t + 1],
                                                         r2[:, t:t + 1], ALU.subtract, ALU.mult)
                            last.then_inc(s_xf, 1)
                        if s == 18:
                            gate_scores(n)
                        if s == 24:
                            gate_pick(n)
                    if a1 is not None:
                        attention(s, a1, a2)
                    if b is not None:
                        if s + AHEAD - 1 < SLOTS:
                            low(b, s + AHEAD - 1)
                        elif a2 is not None:
                            low(a2, s + AHEAD - 1 - SLOTS)
                        if s % KT == KT - 1:
                            weigh(b, s)
                if b is None and a2 is None:
                    split_experts()
                if b is None and a2 is not None:
                    low(a2, 0)
                    low(a2, 1)

            def stats2(base):
                def then(ins, k):
                    ins.then_inc(s_st2, 1)
                    dve.wait_ge(s_st2, base + k)
                mean_e, m2_e, mean_o, m2_o = (bn2[:, :, k] for k in (1, 2, 4, 5))
                then(dve.tensor_tensor(st2[:, 0, :], mean_e, mean_o, ALU.subtract), 2)
                then(dve.tensor_tensor(st2[:, 4, :], mean_e, mean_o, ALU.add), 3)
                then(dve.tensor_tensor(st2[:, 1, :], m2_e, m2_o, ALU.add), 4)
                dve.tensor_scalar(st2[:, 5, :], st2[:, 4, :], 0.5, None, ALU.mult)
                dve.tensor_scalar(st2[:, 1, :], st2[:, 1, :], 1.0 / CH, LN_T_EPS, ALU.mult, ALU.add).then_inc(s_st2, 1)
                then(dve.scalar_tensor_tensor(out=st2[:, 2, :], in0=st2[:, 0, :], scalar=0.25, in1=st2[:, 0, :],
                                              op0=ALU.mult, op1=ALU.mult), 6)
                dve.tensor_tensor(st2[:, 3, :], st2[:, 1, :], st2[:, 2, :], ALU.add).then_inc(s_st2, 1)

            def stats1(base):
                def then(ins, k):
                    ins.then_inc(s_st1, 1)
                    dve.wait_ge(s_st1, base + k)
                mean_e, m2_e, mean_o, m2_o = (bn1[:, :, k] for k in (1, 2, 4, 5))
                dve.tensor_tensor(st1[:, 0, :], mean_e, mean_o, ALU.subtract)
                then(dve.tensor_tensor(st1[:, 1, :], m2_e, m2_o, ALU.add), 2)
                dve.tensor_scalar(st1[:, 3, :], st1[:, 1, :], 1.0 / CH, RMS_EPS * LN_C_EPS / CH, ALU.mult, ALU.add)
                then(dve.scalar_tensor_tensor(out=st1[:, 2, :], in0=st1[:, 0, :], scalar=0.25, in1=st1[:, 0, :],
                                              op0=ALU.mult, op1=ALU.mult), 3)
                then(dve.tensor_tensor(st1[:, 2, :], st1[:, 2, :], st1[:, 3, :], ALU.add), 4)
                dve.tensor_scalar(st1[:, 4, :], st1[:, 2, :], 1.0 + RMS_EPS / CH, None, ALU.mult).then_inc(s_st1, 1)

            def gate_step(n, k, ins):
                ins.then_inc(s_gate, 1)
                dve.wait_ge(s_gate, n * GATE + k)

            def over_experts(k):
                return gate_stat[:, k, :].unsqueeze(2).broadcast_to((P, TILES, EXPERTS))

            def gate_scores(n):
                logits = ab[:, BANK_OF["L"], 0:TILES * EXPERTS].rearrange("p (t e) -> p t e", e=EXPERTS)
                dve.wait_ge(s_lg_mm, n + 1)
                gate_step(n, 1, dve.tensor_tensor(gate[:, 2, :, :], logits, gate_b_bc[:, :].unsqueeze(1).broadcast_to(
                    (P, TILES, EXPERTS)), ALU.add))
                gate_step(n, 2, dve.tensor_reduce(gate_stat[:, 0, :], gate[:, 2, :, :], X_AXIS, ALU.max))
                dve.tensor_tensor(gate[:, 0, :, :], gate[:, 2, :, :], over_experts(0), ALU.subtract).then_inc(s_gate, 1)

            def gate_pick(n):
                dve.wait_ge(s_gate_exp, n + 1)
                ranks = rank[:, :].unsqueeze(1).broadcast_to((P, TILES, EXPERTS))
                g = lambda k: gate[:, k, :, :]
                gate_step(n, 4, dve.tensor_reduce(gate_stat[:, 1, :], g(1), X_AXIS, ALU.add))
                gate_step(n, 5, dve.reciprocal(gate_stat[:, 2, :], gate_stat[:, 1, :]))
                gate_step(n, 6, dve.tensor_tensor(g(2), g(1), over_experts(2), ALU.mult))
                gate_step(n, 7, dve.tensor_reduce(gate_stat[:, 3, :], g(2), X_AXIS, ALU.max))
                gate_step(n, 8, dve.tensor_tensor(g(3), g(2), over_experts(3), ALU.is_equal))
                gate_step(n, 9, dve.tensor_tensor(g(3), g(3), ranks, ALU.mult))
                gate_step(n, 10, dve.tensor_reduce(gate_stat[:, 4, :], g(3), X_AXIS, ALU.max))
                gate_step(n, 11, dve.tensor_tensor(g(3), g(3), over_experts(4), ALU.is_equal))
                gate_step(n, 12, dve.scalar_tensor_tensor(out=g(4), in0=g(3), scalar=-2.0, in1=g(2),
                                                          op0=ALU.mult, op1=ALU.add))
                gate_step(n, 13, dve.tensor_reduce(gate_stat[:, 5, :], g(4), X_AXIS, ALU.max))
                gate_step(n, 14, dve.tensor_tensor(g(5), g(4), over_experts(5), ALU.is_equal))
                gate_step(n, 15, dve.tensor_tensor(g(5), g(5), ranks, ALU.mult))
                gate_step(n, 16, dve.tensor_reduce(gate_stat[:, 6, :], g(5), X_AXIS, ALU.max))
                gate_step(n, 17, dve.tensor_tensor(g(5), g(5), over_experts(6), ALU.is_equal))
                gate_step(n, 18, dve.tensor_tensor(g(3), g(3), g(5), ALU.add))
                wait(dve, s_cw_mm, n)
                dve.tensor_tensor(cw_tok[:, 0, :, :].rearrange("p e t -> p t e"), g(3), g(2), ALU.mult).then_inc(s_gate, 1)

            def attention(s, a1, a2):
                n = a1.index
                if s in (10, 12):
                    h = (s - 10) // 2
                    dve.wait_ge(s_x_tok, n * 2 + h + 1)
                    if h == 0:
                        wait(dve, s_r1, n)
                    for t in range(h * HT, (h + 1) * HT):
                        last = dve.bn_stats(bn1[:, t, :], x_tok[:, a1.parity, t, :])
                if s == 12:
                    last.then_inc(s_st1, 1)
                    dve.wait_ge(s_st1, n * ST1 + 1)
                    stats1(n * ST1)
                if s in (14, 15, 16, 17):
                    for t in (2 * (s - 14), 2 * (s - 14) + 1):
                        if t == 0:
                            dve.wait_ge(s_r1, n + 1)
                            wait(dve, s_c_mm, n)
                            wait(dve, s_q_tr, n * 2)
                        dve.wait_ge(s_qkv_mm, n * TILES + t + 1)
                        bank = BANK_OF[f"Q{t}"]
                        dve.tensor_scalar(qkv[:, t, :], ab[:, bank, 0:3 * P], r1[:, t:t + 1], None,
                                          ALU.mult).then_inc(s_qkv, 1)
                if s == 19:
                    dve.wait_ge(s_qkv, n * TILES + TILES)
                    dve.tensor_reduce(q_stat[:, 0, :].rearrange("p (t h) -> p t h", h=HEADS),
                                      qkv[:, :, 0:P].rearrange("p t (h d) -> p t h d", d=HEAD_DIM),
                                      X_AXIS, ALU.max).then_inc(s_q_max, 1)
                if s == 20:
                    wait(dve, s_kt_mm, n)
                    dve.tensor_reduce(k_part[:, :], qkv[:, :, P:2 * P].rearrange("p t c -> p c t"),
                                      X_AXIS, ALU.max).then_inc(s_k_part, 1)
                if s == 21:
                    dve.wait_ge(s_kt_mm, n + 1)
                    dve.tensor_reduce(k_max[:, :], ab[:, BANK_OF["KT"], 0:P], X_AXIS, ALU.max).then_inc(s_k_max, 1)
                    dve.wait_ge(s_k_max, n * 2 + 1)
                    dve.tensor_scalar(k_diag[:, :], ident[:, :], k_max[:, 0:1], None, ALU.mult).then_inc(s_k_max, 1)
                if s == 22:
                    dve.wait_ge(s_kb_mm, n + 1)
                    k = qkv[:, :, P:2 * P]
                    dve.tensor_tensor(k, k, ab[:, BANK_OF["KB"], 0:P].unsqueeze(1).broadcast_to((P, TILES, P)),
                                      ALU.subtract).then_inc(s_k_sub, 1)
                if s == 25:
                    dve.wait_ge(s_exp, n * 2 + 1)
                    dve.tensor_reduce(q_stat[:, 1, :].rearrange("p (t h) -> p t h", h=HEADS),
                                      qkv[:, :, 0:P].rearrange("p t (h d) -> p t h d", d=HEAD_DIM),
                                      X_AXIS, ALU.add).then_inc(s_q_sum, 1)
                    dve.wait_ge(s_q_sum, n * 2 + 1)
                    dve.reciprocal(q_stat[:, 2, :], q_stat[:, 1, :]).then_inc(s_q_sum, 1)
                if s == 27:
                    dve.wait_ge(s_c_mm, n + 1)
                    wait(dve, s_m_mm, n)
                    wait(dve, s_mix, n)
                    dve.tensor_tensor(ctx_t[:, :], ab[:, BANK_OF["C"], 0:P], head_mask[:, :], ALU.mult).then_inc(s_ctx, 1)
                    dve.reciprocal(k_recip[:, :], ab[:, BANK_OF["C"], P:P + 1]).then_inc(s_ctx, 1)
                if s == 29:
                    dve.wait_ge(s_m_mm, n + 1)
                    wait(dve, s_fin, (n - 1) * 2)
                    dve.scalar_tensor_tensor(out=mix[:, a1.parity, :], in0=ab[:, BANK_OF["M"], 0:P],
                                             scalar=k_recip[:, 0:1], in1=b_out_bc[:, :], op0=ALU.mult,
                                             op1=ALU.add).then_inc(s_mix, 1)

            run(dve, body)

        @block.tensor
        def _(pe):
            def parts(out_ap, lhs, rhs, start, stop):
                (lh, ll), (rh, rl) = lhs, rhs
                pe.matmul(out_ap, lh, rh, start=start, stop=False)
                pe.matmul(out_ap, ll, rh, start=False, stop=False)
                return pe.matmul(out_ap, lh, rl, start=False, stop=stop)

            def up(b, s):
                e, k, h = s // KT % EXPERTS, s % KT, s // UNITS
                if s == 0:
                    pe.wait_ge(s_xf_split, b.index * 2 + 2)
                cols = slice(h * HALF, (h + 1) * HALF)
                rows = slice(k * P, (k + 1) * P)
                parts(hidden_ps[:, s % HB, :], (w1h[:, e, rows], w1l[:, e, rows]),
                      (xfh[:, b.parity, cols], xfl[:, b.parity, cols]), True, True).then_inc(s_up, 1)

            def down(b, s):
                u, e, k = s // KT, s // KT % EXPERTS, s % KT
                if k == 0:
                    pe.wait_ge(s_weighted, b.index * UNITS + u - 1 + CREDIT)
                pe.wait_ge(s_lo, b.index * SLOTS + s + 1)
                last = parts(y_ps[:, u % 2, :], (w2h[:, e * KT + k, :], w2l[:, e * KT + k, :]),
                             (gh[:, s % HB, :], gl[:, s % HB, :]), k == 0, k == KT - 1)
                if k == KT - 1:
                    last.then_inc(s_down, 1)

            pe.wait_ge(s_wqkv, 6)
            pe.wait_ge(s_ident, 2)
            pe.wait_ge(s_const, POOL_CONSTS)
            for j in range(3):
                last = pe.transpose(ab[:, 0, j * P:(j + 1) * P], wqkv_raw[:, j, :], ident[:, :])
            last.then_inc(s_wtr, 1)
            pe.wait_ge(s_load_small, 16 * 7)
            n = EXPERTS * KT
            pe.transpose(ab[:, 1, 0:P], w_out_raw[:, :], ident[:, :])
            pe.transpose(ab[:, 1, P:P + n], b1_raw[:, :], ident[0:n, 0:n])
            pe.transpose(ab[:, 1, P + n:P + n + EXPERTS], b2_raw[:, :],
                         ident[0:EXPERTS, 0:EXPERTS]).then_inc(s_wtr, 1)
            pe.wait_ge(s_wready, WREADY)

            def body(b, a1, a2):
                def claim(name):
                    s, count = last_read_of(name, a1, a2)
                    wait(pe, s, count)
                    return ab[:, BANK_OF[name], :]

                def turn(name, src, done):
                    bank = claim(name)
                    for k in range(HT):
                        last = pe.transpose(bank[:, k * P:(k + 1) * P], src(k), ident[:, :])
                    last.then_inc(done, 1)

                for s in range(SLOTS):
                    if a2 is not None:
                        n = a2.index
                        if s in (0, 1):
                            if s == 0:
                                pe.wait_ge(s_mix, n + 1)
                                pe.wait_ge(s_q_ch, n * 2 + 2)
                            bank = claim(f"F{s}")
                            for k in range(HT):
                                t = s * HT + k
                                last = pe.matmul(bank[:, k * P:(k + 1) * P], q_ch[:, a2.parity, t * P:(t + 1) * P],
                                                 mix[:, a2.parity, :], start=True, stop=True)
                            last.then_inc(s_fin, 1)
                        if s in (9, 10):
                            if s == 9:
                                pe.wait_ge(s_x1, n + 1)
                            turn(f"O{s - 9}", lambda k: x1_tok[:, (s - 9) * HT + k, :], s_o_tr)
                        if s in (12, 13):
                            if s == 12:
                                pe.wait_ge(s_xf, n + 1)
                            turn(f"G{s - 12}", lambda k: xf_tok[:, (s - 12) * HT + k, :], s_g_tr)
                        if s == 18:
                            pe.wait_ge(s_xf_ch, n * 2 + 2)
                            bank = claim("L")
                            for t in range(TILES):
                                last = pe.matmul(bank[:, t * EXPERTS:(t + 1) * EXPERTS], xf_ch[:, t * P:(t + 1) * P],
                                                 gate_w_sb[:, :], start=True, stop=True)
                            last.then_inc(s_lg_mm, 1)
                        if s == 25:
                            pe.wait_ge(s_gate, n * GATE + GATE)
                            pe.transpose(claim("CW")[:, 0:P],
                                         cw_tok[:, :, :, :].rearrange("p a e t -> p (a e t)"), ident[:, :]).then_inc(s_cw_mm, 1)
                    if a1 is not None:
                        n = a1.index
                        if s in (7, 8):
                            if s == 7:
                                pe.wait_ge(s_x_in[a1.parity], a1.pair * 16 + 16)
                            turn(f"X{s - 7}", lambda k: x_sb[:, a1.parity, ((s - 7) * HT + k) * P:((s - 7) * HT + k + 1) * P],
                                 s_x_tr)
                        if s in (14, 15, 16, 17):
                            if s == 14:
                                pe.wait_ge(s_x_split, n * 2 + 2)
                            for t in (2 * (s - 14), 2 * (s - 14) + 1):
                                cols = slice(t * P, (t + 1) * P)
                                parts(claim(f"Q{t}")[:, 0:3 * P], (xh[:, cols], xl[:, cols]),
                                      (wqkv_h[:, :], wqkv_l[:, :]), True, True).then_inc(s_qkv_mm, 1)
                        if s == 20:
                            pe.wait_ge(s_k_part, n + 1)
                            pe.transpose(claim("KT")[:, 0:P], k_part[:, :], ident[:, :]).then_inc(s_kt_mm, 1)
                        if s == 22:
                            pe.wait_ge(s_k_max, n * 2 + 2)
                            pe.matmul(claim("KB")[:, 0:P], ones[:, :], k_diag[:, :], start=True,
                                      stop=True).then_inc(s_kb_mm, 1)
                        if s == 26:
                            pe.wait_ge(s_exp, n * 2 + 2)
                            bank = claim("C")
                            for t in range(TILES):
                                pe.matmul(bank[:, 0:P], qkv[:, t, 2 * P:3 * P], qkv[:, t, P:2 * P],
                                          start=t == 0, stop=t == TILES - 1)
                            for t in range(TILES):
                                last = pe.matmul(bank[:, P:P + 2], qkv[:, t, P:2 * P], ones[:, 0:2],
                                                 start=t == 0, stop=t == TILES - 1)
                            last.then_inc(s_c_mm, 1)
                        if s == 28:
                            pe.wait_ge(s_ctx, n * 2 + 1)
                            pe.matmul(claim("M")[:, 0:P], ctx_t[:, :], w_out_t[:, :], start=True,
                                      stop=True).then_inc(s_m_mm, 1)
                        if s in (27, 28):
                            if s == 27:
                                pe.wait_ge(s_q_norm, n + 1)
                            turn(f"T{s - 27}", lambda k: qkv[:, (s - 27) * HT + k, 0:P], s_q_tr)
                    if b is not None:
                        if s + AHEAD < SLOTS:
                            up(b, s + AHEAD)
                        elif a2 is not None:
                            up(a2, s + AHEAD - SLOTS)
                        down(b, s)
                if b is None and a2 is not None:
                    pe.wait_ge(s_wsplit, 4)
                    for s in range(AHEAD):
                        up(a2, s)

            run(pe, body)


_INS = ['x', 'L0_conv_W_qkv', 'L0_conv_W_out', 'L0_conv_b_out', 'L0_conv_g_norm', 'L0_conv_g_out',
        'L0_ffn_gate_w', 'L0_ffn_gate_b', 'L0_ffn_W1', 'L0_ffn_b1', 'L0_ffn_W2', 'L0_ffn_b2']
_OUTS = [((16, 128, 32, 32), 'float32')]


def kernel(**inputs):
    import numpy as _np
    import concourse.bacc as _bacc
    from concourse import mybir as _mybir
    from concourse.bass_utils import run_bass_kernel_spmd as _run

    nc = _bacc.Bacc("TRN2", target_bir_lowering=False, num_devices=1)
    arrays, args = {}, []
    for name in _INS:
        a = _np.ascontiguousarray(inputs[name])
        arrays[f"in_{name}_dram"] = a
        args.append(nc.dram_tensor(f"in_{name}_dram", a.shape, _mybir.dt.from_np(a.dtype), kind="ExternalInput").ap())
    for i, (shape, dtype) in enumerate(_OUTS):
        dt = _mybir.dt.from_np(_np.dtype(dtype))
        args.append(nc.dram_tensor(f"out_{i}_dram", shape, dt, kind="ExternalOutput").ap())
    build(nc, *args)
    r = _run(nc, [arrays], core_ids=[0])
    got = tuple(r.results[0][f"out_{i}_dram"] for i in range(len(_OUTS)))
    return got[0]
```

```python
from contextlib import ExitStack

import concourse.bass as bass
from concourse import mybir

ALU = mybir.AluOpType
ACT = mybir.ActivationFunctionType
X_AXIS = mybir.AxisListType.X
F32 = mybir.dt.float32
F32R = mybir.dt.float32r

P = 128
BATCH, CH, TOK = 16, 128, 1024
TILES = TOK // P
HALF = TOK // 2
HT = HALF // P
HEADS, HEAD_DIM = 4, 32
EXPERTS, HIDDEN = 8, 256
KT = HIDDEN // P
SLOTS = 2 * EXPERTS * KT
UNITS = 2 * EXPERTS
AHEAD = 3
LOW_AHEAD = 2
WB = 4
HB = 4
LN_C_EPS, LN_T_EPS, RMS_EPS = 1e-6, 1e-5, 1e-12

PE_SLOT = {"F0": 0, "F1": 1, "X0": 8, "O0": 8, "X1": 10, "O1": 11, "G0": 12, "G1": 12, "Q0": 16, "Q1": 16,
           "Q2": 17, "Q3": 17, "Q4": 17, "Q5": 17, "Q6": 17, "Q7": 17, "L": 20, "KT": 20, "KB": 23, "C": 26,
           "W": 28, "M": 29, "T0": 29, "T1": 29}
ACT_SLOT = {"square0": 0, "square1": 1, "x_tok0": 7, "x_tok1": 9, "x1_ch0": 9, "x1_ch1": 10, "xf_ch0": 13,
            "xf_ch1": 14, "exp": 23, "cw_rows": 28, "q_ch0": 28, "q_ch1": 29}
DVE_SLOT = {"ss0": 1, "ss1": 2, "norm0": 4, "norm1": 4, "bn2_0": 8, "bn2_1": 8, "xf": 10, "bn1_0": 11,
            "bn1_1": 11, "qkv0": 16, "qkv1": 16, "qkv2": 17, "qkv3": 17, "qkv4": 17, "qkv5": 17, "qkv6": 17,
            "qkv7": 17, "k_part": 19, "scores": 20, "q_max": 20, "k_max": 20, "k_shift": 23, "pick0": 24,
            "pick1": 24, "pick2": 24, "q_sum": 25, "ctx": 28, "mix": 29}
POOL_SLOT = {"rms": 1, "x_high": 7, "x1": 7, "r2": 7, "x_low": 8, "r1": 11, "xf_high": 13, "xf_low": 14,
             "q_shift": 21, "q_norm": 26}
STAGE_2 = ("F0", "F1", "O0", "O1", "G0", "G1", "L", "W")

BANK_USES = [(name, n % 2, 2 if name in STAGE_2 else 1) for n, name in enumerate(
    sorted(PE_SLOT, key=lambda name: (PE_SLOT[name], name not in STAGE_2, list(PE_SLOT).index(name))))]
BANK_OF = {name: bank for name, bank, _ in BANK_USES}


class Image:

    def __init__(self, pair, parity):
        self.pair, self.parity = pair, parity
        self.index = pair * 2 + parity

    def plus(self, n):
        return Image(self.pair + (self.parity + n) // 2, (self.parity + n) % 2)


def wait(eng, sem, value):
    if not isinstance(value, int) or value > 0:
        eng.wait_ge(sem, value)


def build(nc, x, w_qkv, w_out, b_out, g_norm, g_out, gate_w, gate_b, w1, b1, w2, b2, out):
    x_dram = x.rearrange("b c h w -> (b c) (h w)")
    out_dram = out.rearrange("b c h w -> (b c) (h w)")
    w1_dram = w1.rearrange("e c h -> c e h")
    w2_dram = w2.rearrange("e (k p) d -> p (e k) d", p=P)
    scratch = nc.dram_tensor("routing_scratch", [2 * EXPERTS * TILES, P], F32, kind="Internal").ap()

    with ExitStack() as ctx:
        def sb(name, shape, dt=F32):
            return ctx.enter_context(nc.sbuf_tensor(name, shape, dt))

        def sem(name):
            return ctx.enter_context(nc.semaphore(name))

        hidden_ps = ctx.enter_context(nc.psum_tensor("hidden_ps", [P, HB, HALF], F32))
        y_ps = ctx.enter_context(nc.psum_tensor("y_ps", [P, 2, HALF], F32))
        ab = ctx.enter_context(nc.psum_tensor("ab", [P, 2, HALF], F32))

        ident = sb("ident", [P, P])
        ones = sb("ones", [P, P])
        head_mask = sb("head_mask", [P, P])
        minus_half = sb("minus_half", [P, TILES])
        rms_eps = sb("rms_eps", [P, TILES])
        turn_in, turn_out = sb("turn_in", [P, 1]), sb("turn_out", [P, 1])
        rank = sb("rank", [P, EXPERTS])
        g_norm_bc = sb("g_norm_bc", [P, P])
        g_out_bc = sb("g_out_bc", [P, P])
        b_out_bc = sb("b_out_bc", [P, P])
        gate_b_bc = sb("gate_b_bc", [P, EXPERTS])
        gate_w_sb = sb("gate_w_sb", [P, EXPERTS])
        w_mean = sb("w_mean", [P, 3])
        w_out_raw = sb("w_out_raw", [P, P])
        b1_raw = sb("b1_raw", [EXPERTS * KT, P])
        b2_raw = sb("b2_raw", [EXPERTS, P])
        wqkv_h = sb("wqkv_h", [P, 3 * P], F32R)
        wqkv_l = sb("wqkv_l", [P, 3 * P], F32R)
        w_out_t = sb("w_out_t", [P, P])
        b1_t = sb("b1_t", [P, EXPERTS * KT])
        b2_t = sb("b2_t", [P, EXPERTS])
        w1h = sb("w1h", [P, EXPERTS, HIDDEN], F32R)
        w1l = sb("w1l", [P, EXPERTS, HIDDEN], F32R)
        w2h = sb("w2h", [P, EXPERTS * KT, CH], F32R)
        w2l = sb("w2l", [P, EXPERTS * KT, CH], F32R)

        x_sb = sb("x_sb", [P, 2, TOK])
        xh = sb("xh", [P, TOK], F32R)
        xl = sb("xl", [P, TOK], F32R)
        x_tok = sb("x_tok", [P, 2, TILES, CH])
        bn1 = sb("bn1", [P, TILES, 6])
        st1 = sb("st1", [P, 5, TILES])
        r1 = sb("r1", [P, TILES])
        qkv = sb("qkv", [P, TILES, 3 * P])
        q_stat = sb("q_stat", [P, 3, TILES * HEADS])
        k_part = sb("k_part", [P, P])
        k_max = sb("k_max", [P, 1])
        k_diag = sb("k_diag", [P, P])
        ctx_t = sb("ctx_t", [P, P])
        k_recip = sb("k_recip", [P, 1])
        mix = sb("mix", [P, 2, P])
        q_ch = sb("q_ch", [P, 2, TOK])

        square = sb("square", [P, 2, HALF])
        ss = sb("ss", [P, 2, TILES])
        r_rms = sb("r_rms", [P, TILES])
        x1_tok = sb("x1_tok", [P, TILES, CH])
        bn2 = sb("bn2", [P, TILES, 6])
        st2 = sb("st2", [P, 6, TILES])
        r2 = sb("r2", [P, TILES])
        xf_tok = sb("xf_tok", [P, TILES, CH])
        x1_ch = sb("x1_ch", [P, 2, TOK])
        xf_ch = sb("xf_ch", [P, TOK])
        xfh = sb("xfh", [P, 2, TOK], F32R)
        xfl = sb("xfl", [P, 2, TOK], F32R)
        gate = sb("gate", [P, 6, TILES, EXPERTS])
        gate_stat = sb("gate_stat", [P, 7, TILES])
        cw_tok = sb("cw_tok", [P, 2, EXPERTS, TILES])
        cw_rows = sb("cw_rows", [EXPERTS * TILES, P])
        cw = sb("cw", [P, 2, EXPERTS, HALF])

        gh = sb("gh", [P, HB, HALF], F32R)
        gl = sb("gl", [P, HB, HALF], F32R)
        weighted = sb("weighted", [P, WB, HALF])

        wqkv_raw = cw[:, 0, 0, 0:3 * P].rearrange("p (j c) -> p j c", j=3)
        wqkv_c = cw[:, 0, 1, 0:3 * P].rearrange("p (j c) -> p j c", j=3)
        w1_raw = cw[:, 1, 0:4, :].rearrange("p a n -> p (a n)")
        w2_raw = cw[:, 1, 4:8, :].rearrange("p a n -> p (a n)")

        s_load_qkv, s_load_small, s_load_experts = sem("load_qkv"), sem("load_small"), sem("load_experts")
        s_const, s_ident = sem("const_done"), sem("ident_done")
        s_wqkv, s_wtr, s_wready = sem("wqkv_centered"), sem("weights_transposed"), sem("weights_ready")
        s_wsplit = sem("expert_weights_split")
        s_x_in = [sem("x_in0"), sem("x_in1")]
        s_x_split = sem("x_split")
        s_x_tr = sem("x_transposed")
        s_x_tok = sem("x_tok_done")
        s_st1 = sem("stats1_step")
        s_r1 = sem("r1_done")
        s_qkv_mm, s_qkv = sem("qkv_product"), sem("qkv_scaled")
        s_q_max, s_k_part = sem("q_max"), sem("k_part_max")
        s_q_sub, s_k_sub = sem("q_shifted"), sem("k_shifted")
        s_kt_mm, s_k_max, s_kb_mm = sem("k_max_transposed"), sem("k_max_step"), sem("k_max_spread")
        s_exp = sem("exp_done")
        s_q_sum, s_q_norm = sem("q_sum_step"), sem("q_normalised")
        s_c_mm, s_ctx, s_m_mm, s_mix = sem("context"), sem("context_step"), sem("mix_product"), sem("mix_done")
        s_q_tr, s_q_ch = sem("q_transposed"), sem("q_ch_done")
        s_fin, s_square, s_ss = sem("attention_out"), sem("square_done"), sem("square_sum")
        s_rms, s_y, s_x1 = sem("rms_step"), sem("normed_out"), sem("x1_done")
        s_st2, s_r2, s_xf = sem("stats2_step"), sem("r2_done"), sem("xf_done")
        s_o_tr, s_x1_ch = sem("x1_transposed"), sem("x1_ch_done")
        s_g_tr, s_xf_ch = sem("xf_transposed"), sem("xf_ch_done")
        s_xf_split = sem("xf_split")
        s_lg_mm, s_gate, s_gate_exp = sem("logits"), sem("gate_step"), sem("gate_exp")
        s_cw_mm, s_cw_rows, s_scratch = sem("cw_transposed"), sem("cw_rows_done"), sem("cw_in_dram")
        s_cw_in = [[sem(f"cw_in{h}{q}") for q in range(2)] for h in range(2)]
        s_up, s_gelu, s_lo = sem("up_done"), sem("gelu_done"), sem("low_done")
        s_down, s_weighted, s_added = sem("down_done"), sem("weighted_done"), sem("added_done")
        s_out = [[sem(f"stored{p}{h}") for h in range(2)] for p in range(2)]

        ST1, ST2, GATE = 5, 7, 19
        WREADY = 7
        POOL_CONSTS = 4 + EXPERTS
        CREDIT, STORE_CREDIT = 4, 16

        READ_OUT = {"F0": (s_y, 2, 1), "F1": (s_y, 2, 2), "X0": (s_x_tok, 2, 1), "X1": (s_x_tok, 2, 2),
                    "O0": (s_x1_ch, 2, 1), "O1": (s_x1_ch, 2, 2), "G0": (s_xf_ch, 2, 1), "G1": (s_xf_ch, 2, 2),
                    "L": (s_gate, GATE, 1), "KT": (s_k_max, 2, 1), "KB": (s_k_sub, 1, 1), "W": (s_cw_rows, 1, 1),
                    "C": (s_ctx, 2, 2), "T0": (s_q_ch, 2, 1), "M": (s_mix, 1, 1), "T1": (s_q_ch, 2, 2)}
        READ_OUT.update({f"Q{t}": (s_qkv, TILES, t + 1) for t in range(TILES)})

        def last_read_of(name, a1, a2):
            order = [n for n, bank, _ in BANK_USES if bank == BANK_OF[name]]
            stage = {n: st for n, _, st in BANK_USES}
            image = {1: a1, 2: a2}
            for n in reversed(order[:order.index(name)]):
                if image[stage[n]] is not None:
                    s, per, k = READ_OUT[n]
                    return s, image[stage[n]].index * per + k
            s, per, k = READ_OUT[order[-1]]
            before = (a1.index if a1 is not None else BATCH) - 1
            return s, before * per + k

        def run(eng, body):
            body(None, Image(0, 0), None)
            body(None, Image(0, 1), Image(0, 0))
            with eng.Fori(0, BATCH // 2 - 1) as pair:
                for parity in range(2):
                    b = Image(pair, parity)
                    body(b, b.plus(2), b.plus(1))
            body(Image(BATCH // 2 - 1, 0), None, Image(BATCH // 2 - 1, 1))
            body(Image(BATCH // 2 - 1, 1), None, None)

        block = ctx.enter_context(nc.Block())

        @block.sync
        def _(sp):
            def load_x(a):
                wait(sp, s_x_split, (a.index - 1) * 2)
                wait(sp, s_x_tr, (a.index - 1) * 2)
                sp.dma_start(x_sb[:, a.parity, :], x_dram[bass.ds(a.index * P, P), :]).then_inc(s_x_in[a.parity], 16)

            sp.dma_start(wqkv_raw, w_qkv.rearrange("(j o) c -> o j c", j=3)).then_inc(s_load_qkv, 16)
            sp.dma_start(g_norm_bc[:, :], g_norm.partition_broadcast(P)).then_inc(s_load_qkv, 16)
            load_x(Image(0, 0))
            sp.dma_start(w1_raw.rearrange("p (e h) -> p e h", e=EXPERTS), w1_dram).then_inc(s_load_experts, 16)
            sp.dma_start(w2_raw.rearrange("p (e d) -> p e d", d=CH), w2_dram).then_inc(s_load_experts, 16)

            def body(b, a1, a2):
                if a1 is not None and not (b is None and a2 is None):
                    load_x(a1)
                if b is not None:
                    store(b, 0)
                if a2 is not None:
                    rows = EXPERTS * TILES
                    wait(sp, s_cw_rows, a2.index + 1)
                    sp.dma_start(scratch[a2.parity * rows:(a2.parity + 1) * rows, :], cw_rows[:, :]).then_inc(s_scratch, 16)
                    sp.wait_ge(s_scratch, (a2.index + 1) * 16)
                    for h in range(2):
                        if b is not None:
                            sp.wait_ge(s_weighted, b.index * UNITS + (h + 1) * EXPERTS + CREDIT)
                        elif h == 1:
                            sp.wait_ge(s_wsplit, 4)
                        for q in range(2):
                            half_rows = scratch[a2.parity * rows:(a2.parity + 1) * rows, :].rearrange(
                                "(e t) n -> e t n", e=EXPERTS)[q * 4:q * 4 + 4, h * HT:(h + 1) * HT, :]
                            sp.dma_start(cw[:, h, q * 4:q * 4 + 4, :],
                                         half_rows.rearrange("e t n -> e (t n)").partition_broadcast(P)
                                         ).then_inc(s_cw_in[h][q], 16)
                if b is not None:
                    store(b, 1)

            def store(b, h):
                sp.wait_ge(s_added, b.index * UNITS + (h + 1) * EXPERTS + CREDIT)
                sp.dma_start(out_dram[bass.ds(b.index * P, P), h * HALF:(h + 1) * HALF],
                             x1_ch[:, b.parity, h * HALF:(h + 1) * HALF]).then_inc(s_out[b.parity][h], 16)

            run(sp, body)
            for p in range(2):
                for h in range(2):
                    sp.wait_ge(s_out[p][h], 16 * (BATCH // 2) + STORE_CREDIT)

        @block.gpsimd
        def _(pool):
            def turnstile():
                pool.tensor_tensor(turn_out[:, :], turn_in[:, :], turn_in[:, :], ALU.add)

            pool.memset(ident[:, :], 0.0).then_inc(s_ident, 1)
            pool.memset(ones[:, :], 1.0).then_inc(s_const, 1)
            pool.memset(minus_half[:, :], -0.5).then_inc(s_const, 1)
            pool.memset(rms_eps[:, :], RMS_EPS).then_inc(s_const, 1)
            pool.memset(turn_in[:, :], 0.0).then_inc(s_const, 1)
            pool.memset(weighted[:, 0, 0:1], 0.0).then_inc(s_added, CREDIT)
            for p in range(2):
                for h in range(2):
                    pool.memset(weighted[:, 1, 2 * p + h:2 * p + h + 1], 0.0).then_inc(s_out[p][h], STORE_CREDIT)
            for e in range(EXPERTS):
                pool.memset(rank[:, e:e + 1], float(EXPERTS - e)).then_inc(s_const, 1)
            pool.wait_ge(s_ident, 1)
            pool.affine_select(out=ident[:, :], in_=ident[:, :], compare_op=ALU.not_equal, fill=1.0,
                               base=0, pattern=[[-1, P]], channel_multiplier=1).then_inc(s_ident, 1)
            pool.wait_ge(s_const, POOL_CONSTS)

            def add(b, s):
                u = s // KT
                h = u // EXPERTS
                dst = x1_ch[:, b.parity, h * HALF:(h + 1) * HALF]
                if u % EXPERTS == 0:
                    pool.wait_ge(s_x1_ch, b.index * 2 + h + 1)
                else:
                    pool.wait_ge(s_added, b.index * UNITS + u + CREDIT)
                pool.wait_ge(s_weighted, b.index * UNITS + u + 1 + CREDIT)
                pool.tensor_tensor(dst, dst, weighted[:, u % WB, :], ALU.add).then_inc(s_added, 1)

            def body(b, a1, a2):
                for s in range(SLOTS):
                    if a2 is not None:
                        n = a2.index
                        if s == POOL_SLOT["rms"]:
                            wait(pool, s_y, n * 2)
                            pool.wait_ge(s_ss, n * 2 + 2)
                            pool.tensor_tensor(ss[:, 1, :], ss[:, 0, :], rms_eps[:, :], ALU.add).then_inc(s_rms, 1)
                            pool.wait_ge(s_rms, n * 2 + 1)
                            pool.tensor_tensor(r_rms[:, :], ss[:, 1, :], minus_half[:, :], ALU.pow).then_inc(s_rms, 1)
                        if s == POOL_SLOT["x1"]:
                            pool.wait_ge(s_y, n * 2 + 2)
                            pool.tensor_tensor(x1_tok[:, :, :], x_tok[:, a2.parity, :, :], x1_tok[:, :, :],
                                               ALU.add).then_inc(s_x1, 1)
                        if s == POOL_SLOT["r2"]:
                            pool.wait_ge(s_st2, n * ST2 + ST2)
                            pool.tensor_tensor(r2[:, :], st2[:, 3, :], minus_half[:, :], ALU.pow).then_inc(s_r2, 1)
                        if s == POOL_SLOT["xf_high"]:
                            pool.wait_ge(s_xf_ch, n * 2 + 2)
                            if b is not None:
                                pool.wait_ge(s_up, b.index * SLOTS + AHEAD)
                            turnstile()
                            pool.tensor_scalar(xfh[:, a2.parity, :], xf_ch[:, :], 1.0, None, ALU.mult).then_inc(s_xf_split, 1)
                        if s == POOL_SLOT["xf_low"]:
                            pool.wait_ge(s_xf_split, n * 2 + 1)
                            pool.tensor_tensor(xfl[:, a2.parity, :], xf_ch[:, :],
                                               xfh[:, a2.parity, :].bitcast(F32), ALU.subtract).then_inc(s_xf_split, 1)
                    if a1 is not None:
                        n = a1.index
                        if s == POOL_SLOT["x_high"]:
                            pool.wait_ge(s_x_in[a1.parity], a1.pair * 16 + 16)
                            wait(pool, s_qkv_mm, n * TILES)
                            turnstile()
                            pool.tensor_scalar(xh[:, :], x_sb[:, a1.parity, :], 1.0, None, ALU.mult).then_inc(s_x_split, 1)
                        if s == POOL_SLOT["x_low"]:
                            pool.wait_ge(s_x_split, n * 2 + 1)
                            pool.tensor_tensor(xl[:, :], x_sb[:, a1.parity, :], xh[:, :].bitcast(F32),
                                               ALU.subtract).then_inc(s_x_split, 1)
                        if s == POOL_SLOT["r1"]:
                            wait(pool, s_qkv, n * TILES)
                            pool.wait_ge(s_st1, n * ST1 + ST1)
                            pool.tensor_tensor(r1[:, :], st1[:, 4, :], minus_half[:, :], ALU.pow).then_inc(s_r1, 1)
                        if s == POOL_SLOT["q_shift"]:
                            pool.wait_ge(s_q_max, n + 1)
                            q = qkv[:, :, 0:P].rearrange("p t (h d) -> p t h d", d=HEAD_DIM)
                            m = q_stat[:, 0, :].rearrange("p (t h) -> p t h", h=HEADS).unsqueeze(3).broadcast_to(
                                (P, TILES, HEADS, HEAD_DIM))
                            pool.tensor_tensor(q, q, m, ALU.subtract).then_inc(s_q_sub, 1)
                        if s == POOL_SLOT["q_norm"]:
                            pool.wait_ge(s_q_sum, n * 2 + 2)
                            q = qkv[:, :, 0:P].rearrange("p t (h d) -> p t h d", d=HEAD_DIM)
                            m = q_stat[:, 2, :].rearrange("p (t h) -> p t h", h=HEADS).unsqueeze(3).broadcast_to(
                                (P, TILES, HEADS, HEAD_DIM))
                            pool.tensor_tensor(q, q, m, ALU.mult).then_inc(s_q_norm, 1)
                    if b is not None and s % KT == 1 and s > 1:
                        add(b, s - KT)
                if b is not None:
                    add(b, SLOTS - 1)

            run(pool, body)

        @block.scalar
        def _(act):
            act.dma_start(w_out_raw[:, :], w_out).then_inc(s_load_small, 16)
            act.dma_start(b1_raw[:, :], b1.rearrange("e (k p) -> (e k) p", p=P)).then_inc(s_load_small, 16)
            act.dma_start(b2_raw[:, :], b2).then_inc(s_load_small, 16)
            act.dma_start(g_out_bc[:, :], g_out.partition_broadcast(P)).then_inc(s_load_small, 16)
            act.dma_start(b_out_bc[:, :], b_out.partition_broadcast(P)).then_inc(s_load_small, 16)
            act.dma_start(gate_b_bc[:, :], gate_b.partition_broadcast(P)).then_inc(s_load_small, 16)
            act.dma_start(gate_w_sb[:, :], gate_w).then_inc(s_load_small, 16)

            def gelu(b, s):
                act.wait_ge(s_up, b.index * SLOTS + s + 1)
                bank, bias = hidden_ps[:, s % HB, :], b1_t[:, s % UNITS:s % UNITS + 1]
                act.activation(gh[:, s % HB, :], bank, ACT.Gelu, bias=bias)
                act.activation(bank, bank, ACT.Gelu, bias=bias).then_inc(s_gelu, 1)

            def body(b, a1, a2):
                for s in range(SLOTS):
                    if a2 is not None:
                        n = a2.index
                        for h in [h for h in range(2) if s == ACT_SLOT[f"square{h}"]]:
                            act.wait_ge(s_fin, n * 2 + h + 1)
                            act.activation(square[:, h, :], ab[:, BANK_OF[f"F{h}"], :], ACT.Square).then_inc(s_square, 1)
                        for h in [h for h in range(2) if s == ACT_SLOT[f"x1_ch{h}"]]:
                            if h == 0:
                                for k in range(2):
                                    act.wait_ge(s_out[a2.parity][k], a2.pair * 16 + STORE_CREDIT)
                            act.wait_ge(s_o_tr, n * 2 + h + 1)
                            act.activation(x1_ch[:, a2.parity, h * HALF:(h + 1) * HALF],
                                           ab[:, BANK_OF[f"O{h}"], :], ACT.Copy).then_inc(s_x1_ch, 1)
                        for h in [h for h in range(2) if s == ACT_SLOT[f"xf_ch{h}"]]:
                            act.wait_ge(s_g_tr, n * 2 + h + 1)
                            if h == 0:
                                wait(act, s_xf_split, n * 2)
                                wait(act, s_lg_mm, n)
                            act.activation(xf_ch[:, h * HALF:(h + 1) * HALF], ab[:, BANK_OF[f"G{h}"], :], ACT.Copy).then_inc(s_xf_ch, 1)
                        if s == ACT_SLOT["exp"]:
                            act.wait_ge(s_gate, n * GATE + 3)
                            act.activation(gate[:, 1, :, :], gate[:, 0, :, :], ACT.Exp).then_inc(s_gate_exp, 1)
                        if s == ACT_SLOT["cw_rows"]:
                            wait(act, s_scratch, n * 16)
                            act.wait_ge(s_cw_mm, n + 1)
                            act.activation(cw_rows[:, :], ab[0:EXPERTS * TILES, BANK_OF["W"], 0:P],
                                           ACT.Copy).then_inc(s_cw_rows, 1)
                    if a1 is not None:
                        n = a1.index
                        for h in [h for h in range(2) if s == ACT_SLOT[f"x_tok{h}"]]:
                            if h == 0:
                                wait(act, s_x1, n - 1)
                            act.wait_ge(s_x_tr, n * 2 + h + 1)
                            act.activation(x_tok[:, a1.parity, h * HT:(h + 1) * HT, :].rearrange("p t c -> p (t c)"),
                                           ab[:, BANK_OF[f"X{h}"], :], ACT.Copy).then_inc(s_x_tok, 1)
                        if s == ACT_SLOT["exp"]:
                            for sem_sub, j in ((s_q_sub, 0), (s_k_sub, 1)):
                                act.wait_ge(sem_sub, n + 1)
                                part = qkv[:, :, j * P:(j + 1) * P]
                                act.activation(part, part, ACT.Exp).then_inc(s_exp, 1)
                        for h in [h for h in range(2) if s == ACT_SLOT[f"q_ch{h}"]]:
                            act.wait_ge(s_q_tr, n * 2 + h + 1)
                            if h == 0:
                                wait(act, s_fin, (n - 1) * 2)
                            act.activation(q_ch[:, a1.parity, h * HALF:(h + 1) * HALF], ab[:, BANK_OF[f"T{h}"], :],
                                           ACT.Copy).then_inc(s_q_ch, 1)
                    if b is not None:
                        if s + AHEAD < SLOTS:
                            gelu(b, s + AHEAD)
                        elif a2 is not None:
                            gelu(a2, s + AHEAD - SLOTS)
                if b is None and a2 is not None:
                    act.wait_ge(s_wready, WREADY)
                    for s in range(AHEAD):
                        gelu(a2, s)

            run(act, body)

        @block.vector
        def _(dve):
            for i in range(HEADS):
                rows = slice(i * HEAD_DIM, (i + 1) * HEAD_DIM)
                for j in range(HEADS):
                    dve.memset(head_mask[rows, j * HEAD_DIM:(j + 1) * HEAD_DIM],
                               float(HEAD_DIM) ** -0.5 if i == j else 0.0)
            dve.memset(cw_tok[:, 1, :, :], 0.0)
            dve.memset(w_mean[:, 0:1], 0.0).then_inc(s_weighted, CREDIT)
            dve.wait_ge(s_weighted, CREDIT)
            dve.wait_ge(s_const, POOL_CONSTS)
            dve.wait_ge(s_ident, 2)
            dve.wait_ge(s_load_qkv, 32)
            dve.tensor_tensor(wqkv_c, wqkv_raw, g_norm_bc[:, :].unsqueeze(1).broadcast_to((P, 3, P)),
                              ALU.mult).then_inc(s_wqkv, 1)
            dve.wait_ge(s_wqkv, 1)
            dve.tensor_reduce(w_mean[:, :], wqkv_c, X_AXIS, ALU.add).then_inc(s_wqkv, 1)
            dve.wait_ge(s_wqkv, 2)
            dve.tensor_scalar(w_mean[:, :], w_mean[:, :], 1.0 / CH, None, ALU.mult).then_inc(s_wqkv, 1)
            dve.wait_ge(s_wqkv, 3)
            for j in range(3):
                dve.tensor_scalar(wqkv_raw[:, j, :], wqkv_c[:, j, :], w_mean[:, j:j + 1], None,
                                  ALU.subtract).then_inc(s_wqkv, 1)
            dve.wait_ge(s_load_small, 16 * 7)
            dve.tensor_scalar(g_out_bc[:, :], g_out_bc[:, :], float(CH) ** 0.5, None, ALU.mult).then_inc(s_wready, 1)
            dve.tensor_scalar(b_out_bc[:, :], b_out_bc[:, :], 1.0 / HEADS, None, ALU.mult).then_inc(s_wready, 1)
            dve.wait_ge(s_wtr, 1)
            dve.tensor_copy(wqkv_h[:, :], ab[:, 0, 0:3 * P]).then_inc(s_wready, 1)
            dve.wait_ge(s_wready, 3)
            dve.tensor_tensor(wqkv_l[:, :], ab[:, 0, 0:3 * P], wqkv_h[:, :].bitcast(F32), ALU.subtract).then_inc(s_wready, 1)
            dve.wait_ge(s_wtr, 2)
            dve.tensor_copy(w_out_t[:, :], ab[:, 1, 0:P]).then_inc(s_wready, 1)
            dve.tensor_copy(b1_t[:, :], ab[:, 1, P:P + EXPERTS * KT]).then_inc(s_wready, 1)
            dve.tensor_copy(b2_t[:, :], ab[:, 1, P + 16:P + 16 + EXPERTS]).then_inc(s_wready, 1)

            def split_experts():
                dve.wait_ge(s_load_experts, 32)
                w1f, w2f = (w[:, :, :].rearrange("p e n -> p (e n)") for w in (w1h, w2h))
                dve.tensor_copy(w1f, w1_raw).then_inc(s_wsplit, 1)
                dve.tensor_copy(w2f, w2_raw).then_inc(s_wsplit, 1)
                dve.wait_ge(s_wsplit, 2)
                dve.tensor_tensor(w1l[:, :, :].rearrange("p e n -> p (e n)"), w1_raw, w1f.bitcast(F32),
                                  ALU.subtract).then_inc(s_wsplit, 1)
                dve.tensor_tensor(w2l[:, :, :].rearrange("p e n -> p (e n)"), w2_raw, w2f.bitcast(F32),
                                  ALU.subtract).then_inc(s_wsplit, 1)

            def low(b, s):
                dve.wait_ge(s_gelu, b.index * SLOTS + s + 1)
                dve.tensor_tensor(gl[:, s % HB, :], hidden_ps[:, s % HB, :], gh[:, s % HB, :].bitcast(F32),
                                  ALU.subtract).then_inc(s_lo, 1)

            def weigh(b, s):
                u = s // KT
                h, e = u // EXPERTS, u % EXPERTS
                if e % 4 == 0:
                    dve.wait_ge(s_cw_in[h][e // 4], b.index * 16 + 16)
                dve.wait_ge(s_added, b.index * UNITS + u + 1 - WB + CREDIT)
                dve.wait_ge(s_down, b.index * UNITS + u + 1)
                dve.scalar_tensor_tensor(out=weighted[:, u % WB, :], in0=y_ps[:, u % 2, :], scalar=b2_t[:, e:e + 1],
                                         in1=cw[:, h, e, :], op0=ALU.add, op1=ALU.mult).then_inc(s_weighted, 1)

            def body(b, a1, a2):
                for s in range(SLOTS):
                    if a2 is not None:
                        n = a2.index
                        for h in [h for h in range(2) if s == DVE_SLOT[f"ss{h}"]]:
                            if h == 0:
                                wait(dve, s_rms, n * 2)
                            dve.wait_ge(s_square, n * 2 + h + 1)
                            dve.tensor_reduce(ss[:, 0, h * HT:(h + 1) * HT],
                                              square[:, h, :].rearrange("p (t c) -> p t c", c=CH),
                                              X_AXIS, ALU.add).then_inc(s_ss, 1)
                        for h in [h for h in range(2) if s == DVE_SLOT[f"norm{h}"]]:
                            dve.wait_ge(s_rms, n * 2 + 2)
                            if h == 0:
                                wait(dve, s_o_tr, n * 2)
                                wait(dve, s_xf, n)
                            for t in range(h * HT, (h + 1) * HT):
                                k = t - h * HT
                                last = dve.scalar_tensor_tensor(
                                    out=x1_tok[:, t, :], in0=ab[:, BANK_OF[f"F{h}"], k * P:(k + 1) * P], scalar=r_rms[:, t:t + 1],
                                    in1=g_out_bc[:, :], op0=ALU.mult, op1=ALU.mult)
                            last.then_inc(s_y, 1)
                        for h in [h for h in range(2) if s == DVE_SLOT[f"bn2_{h}"]]:
                            dve.wait_ge(s_x1, n + 1)
                            if h == 0:
                                wait(dve, s_r2, n)
                            for t in range(h * HT, (h + 1) * HT):
                                last = dve.bn_stats(bn2[:, t, :], x1_tok[:, t, :])
                        if s == DVE_SLOT["bn2_1"]:
                            base = n * ST2
                            last.then_inc(s_st2, 1)
                            dve.wait_ge(s_st2, base + 1)
                            stats2(base)
                        if s == DVE_SLOT["xf"]:
                            dve.wait_ge(s_r2, n + 1)
                            wait(dve, s_g_tr, n * 2)
                            for t in range(TILES):
                                last = dve.tensor_scalar(xf_tok[:, t, :], x1_tok[:, t, :], st2[:, 5, t:t + 1],
                                                         r2[:, t:t + 1], ALU.subtract, ALU.mult)
                            last.then_inc(s_xf, 1)
                        if s == DVE_SLOT["scores"]:
                            gate_scores(n)
                        for k in [k for k in range(3) if s == DVE_SLOT[f"pick{k}"]]:
                            gate_pick(n, k)
                    if a1 is not None:
                        attention(s, a1, a2)
                    if b is not None:
                        if s + LOW_AHEAD < SLOTS:
                            low(b, s + LOW_AHEAD)
                        elif a2 is not None:
                            low(a2, s + LOW_AHEAD - SLOTS)
                        if s % KT == KT - 1:
                            weigh(b, s)
                if b is None and a2 is None:
                    split_experts()
                if b is None and a2 is not None:
                    for s in range(LOW_AHEAD):
                        low(a2, s)

            def stats2(base):
                def then(ins, k):
                    ins.then_inc(s_st2, 1)
                    dve.wait_ge(s_st2, base + k)
                mean_e, m2_e, mean_o, m2_o = (bn2[:, :, k] for k in (1, 2, 4, 5))
                then(dve.tensor_tensor(st2[:, 0, :], mean_e, mean_o, ALU.subtract), 2)
                then(dve.tensor_tensor(st2[:, 4, :], mean_e, mean_o, ALU.add), 3)
                then(dve.tensor_tensor(st2[:, 1, :], m2_e, m2_o, ALU.add), 4)
                dve.tensor_scalar(st2[:, 5, :], st2[:, 4, :], 0.5, None, ALU.mult)
                dve.tensor_scalar(st2[:, 1, :], st2[:, 1, :], 1.0 / CH, LN_T_EPS, ALU.mult, ALU.add).then_inc(s_st2, 1)
                then(dve.scalar_tensor_tensor(out=st2[:, 2, :], in0=st2[:, 0, :], scalar=0.25, in1=st2[:, 0, :],
                                              op0=ALU.mult, op1=ALU.mult), 6)
                dve.tensor_tensor(st2[:, 3, :], st2[:, 1, :], st2[:, 2, :], ALU.add).then_inc(s_st2, 1)

            def stats1(base):
                def then(ins, k):
                    ins.then_inc(s_st1, 1)
                    dve.wait_ge(s_st1, base + k)
                mean_e, m2_e, mean_o, m2_o = (bn1[:, :, k] for k in (1, 2, 4, 5))
                dve.tensor_tensor(st1[:, 0, :], mean_e, mean_o, ALU.subtract)
                then(dve.tensor_tensor(st1[:, 1, :], m2_e, m2_o, ALU.add), 2)
                dve.tensor_scalar(st1[:, 3, :], st1[:, 1, :], 1.0 / CH, RMS_EPS * LN_C_EPS / CH, ALU.mult, ALU.add)
                then(dve.scalar_tensor_tensor(out=st1[:, 2, :], in0=st1[:, 0, :], scalar=0.25, in1=st1[:, 0, :],
                                              op0=ALU.mult, op1=ALU.mult), 3)
                then(dve.tensor_tensor(st1[:, 2, :], st1[:, 2, :], st1[:, 3, :], ALU.add), 4)
                dve.tensor_scalar(st1[:, 4, :], st1[:, 2, :], 1.0 + RMS_EPS / CH, None, ALU.mult).then_inc(s_st1, 1)

            def gate_step(n, k, ins):
                ins.then_inc(s_gate, 1)
                dve.wait_ge(s_gate, n * GATE + k)

            def over_experts(k):
                return gate_stat[:, k, :].unsqueeze(2).broadcast_to((P, TILES, EXPERTS))

            def gate_scores(n):
                logits = ab[:, BANK_OF["L"], 0:TILES * EXPERTS].rearrange("p (t e) -> p t e", e=EXPERTS)
                dve.wait_ge(s_lg_mm, n + 1)
                gate_step(n, 1, dve.tensor_tensor(gate[:, 2, :, :], logits, gate_b_bc[:, :].unsqueeze(1).broadcast_to(
                    (P, TILES, EXPERTS)), ALU.add))
                gate_step(n, 2, dve.tensor_reduce(gate_stat[:, 0, :], gate[:, 2, :, :], X_AXIS, ALU.max))
                dve.tensor_tensor(gate[:, 0, :, :], gate[:, 2, :, :], over_experts(0), ALU.subtract).then_inc(s_gate, 1)

            def gate_pick(n, part):
                ranks = rank[:, :].unsqueeze(1).broadcast_to((P, TILES, EXPERTS))
                g = lambda k: gate[:, k, :, :]
                if part == 0:
                    dve.wait_ge(s_gate_exp, n + 1)
                    gate_step(n, 4, dve.tensor_reduce(gate_stat[:, 1, :], g(1), X_AXIS, ALU.add))
                    gate_step(n, 5, dve.reciprocal(gate_stat[:, 2, :], gate_stat[:, 1, :]))
                    gate_step(n, 6, dve.tensor_tensor(g(2), g(1), over_experts(2), ALU.mult))
                if part == 1:
                    gate_step(n, 7, dve.tensor_reduce(gate_stat[:, 3, :], g(2), X_AXIS, ALU.max))
                    gate_step(n, 8, dve.tensor_tensor(g(3), g(2), over_experts(3), ALU.is_equal))
                    gate_step(n, 9, dve.tensor_tensor(g(3), g(3), ranks, ALU.mult))
                    gate_step(n, 10, dve.tensor_reduce(gate_stat[:, 4, :], g(3), X_AXIS, ALU.max))
                    gate_step(n, 11, dve.tensor_tensor(g(3), g(3), over_experts(4), ALU.is_equal))
                if part == 2:
                    gate_step(n, 12, dve.scalar_tensor_tensor(out=g(4), in0=g(3), scalar=-2.0, in1=g(2),
                                                              op0=ALU.mult, op1=ALU.add))
                    gate_step(n, 13, dve.tensor_reduce(gate_stat[:, 5, :], g(4), X_AXIS, ALU.max))
                    gate_step(n, 14, dve.tensor_tensor(g(5), g(4), over_experts(5), ALU.is_equal))
                    gate_step(n, 15, dve.tensor_tensor(g(5), g(5), ranks, ALU.mult))
                    gate_step(n, 16, dve.tensor_reduce(gate_stat[:, 6, :], g(5), X_AXIS, ALU.max))
                    gate_step(n, 17, dve.tensor_tensor(g(5), g(5), over_experts(6), ALU.is_equal))
                    gate_step(n, 18, dve.tensor_tensor(g(3), g(3), g(5), ALU.add))
                    wait(dve, s_cw_mm, n)
                    dve.tensor_tensor(cw_tok[:, 0, :, :].rearrange("p e t -> p t e"), g(3), g(2), ALU.mult).then_inc(s_gate, 1)

            def attention(s, a1, a2):
                n = a1.index
                for h in [h for h in range(2) if s == DVE_SLOT[f"bn1_{h}"]]:
                    dve.wait_ge(s_x_tok, n * 2 + h + 1)
                    if h == 0:
                        wait(dve, s_r1, n)
                    for t in range(h * HT, (h + 1) * HT):
                        last = dve.bn_stats(bn1[:, t, :], x_tok[:, a1.parity, t, :])
                if s == DVE_SLOT["bn1_1"]:
                    last.then_inc(s_st1, 1)
                    dve.wait_ge(s_st1, n * ST1 + 1)
                    stats1(n * ST1)
                for t in [t for t in range(TILES) if s == DVE_SLOT[f"qkv{t}"]]:
                    if t == 0:
                        dve.wait_ge(s_r1, n + 1)
                        wait(dve, s_c_mm, n)
                        wait(dve, s_q_tr, n * 2)
                    dve.wait_ge(s_qkv_mm, n * TILES + t + 1)
                    dve.tensor_scalar(qkv[:, t, :], ab[:, BANK_OF[f"Q{t}"], 0:3 * P], r1[:, t:t + 1], None,
                                      ALU.mult).then_inc(s_qkv, 1)
                if s == DVE_SLOT["q_max"]:
                    dve.wait_ge(s_qkv, n * TILES + TILES)
                    dve.tensor_reduce(q_stat[:, 0, :].rearrange("p (t h) -> p t h", h=HEADS),
                                      qkv[:, :, 0:P].rearrange("p t (h d) -> p t h d", d=HEAD_DIM),
                                      X_AXIS, ALU.max).then_inc(s_q_max, 1)
                if s == DVE_SLOT["k_part"]:
                    dve.wait_ge(s_qkv, n * TILES + TILES)
                    wait(dve, s_kt_mm, n)
                    dve.tensor_reduce(k_part[:, :], qkv[:, :, P:2 * P].rearrange("p t c -> p c t"),
                                      X_AXIS, ALU.max).then_inc(s_k_part, 1)
                if s == DVE_SLOT["k_max"]:
                    dve.wait_ge(s_kt_mm, n + 1)
                    dve.tensor_reduce(k_max[:, :], ab[:, BANK_OF["KT"], 0:P], X_AXIS, ALU.max).then_inc(s_k_max, 1)
                    dve.wait_ge(s_k_max, n * 2 + 1)
                    dve.tensor_scalar(k_diag[:, :], ident[:, :], k_max[:, 0:1], None, ALU.mult).then_inc(s_k_max, 1)
                if s == DVE_SLOT["k_shift"]:
                    dve.wait_ge(s_kb_mm, n + 1)
                    k = qkv[:, :, P:2 * P]
                    dve.tensor_tensor(k, k, ab[:, BANK_OF["KB"], 0:P].unsqueeze(1).broadcast_to((P, TILES, P)),
                                      ALU.subtract).then_inc(s_k_sub, 1)
                if s == DVE_SLOT["q_sum"]:
                    dve.wait_ge(s_exp, n * 2 + 1)
                    dve.tensor_reduce(q_stat[:, 1, :].rearrange("p (t h) -> p t h", h=HEADS),
                                      qkv[:, :, 0:P].rearrange("p t (h d) -> p t h d", d=HEAD_DIM),
                                      X_AXIS, ALU.add).then_inc(s_q_sum, 1)
                    dve.wait_ge(s_q_sum, n * 2 + 1)
                    dve.reciprocal(q_stat[:, 2, :], q_stat[:, 1, :]).then_inc(s_q_sum, 1)
                if s == DVE_SLOT["ctx"]:
                    dve.wait_ge(s_c_mm, n + 1)
                    wait(dve, s_m_mm, n)
                    wait(dve, s_mix, n)
                    dve.tensor_tensor(ctx_t[:, :], ab[:, BANK_OF["C"], 0:P], head_mask[:, :], ALU.mult).then_inc(s_ctx, 1)
                    dve.reciprocal(k_recip[:, :], ab[:, BANK_OF["C"], P:P + 1]).then_inc(s_ctx, 1)
                if s == DVE_SLOT["mix"]:
                    dve.wait_ge(s_m_mm, n + 1)
                    wait(dve, s_fin, (n - 1) * 2)
                    dve.scalar_tensor_tensor(out=mix[:, a1.parity, :], in0=ab[:, BANK_OF["M"], 0:P],
                                             scalar=k_recip[:, 0:1], in1=b_out_bc[:, :], op0=ALU.mult,
                                             op1=ALU.add).then_inc(s_mix, 1)

            run(dve, body)

        @block.tensor
        def _(pe):
            def parts(out_ap, lhs, rhs, start, stop):
                (lh, ll), (rh, rl) = lhs, rhs
                pe.matmul(out_ap, lh, rh, start=start, stop=False)
                pe.matmul(out_ap, ll, rh, start=False, stop=False)
                return pe.matmul(out_ap, lh, rl, start=False, stop=stop)

            def up(b, s):
                e, k, h = s // KT % EXPERTS, s % KT, s // UNITS
                if s == 0:
                    pe.wait_ge(s_xf_split, b.index * 2 + 2)
                cols = slice(h * HALF, (h + 1) * HALF)
                rows = slice(k * P, (k + 1) * P)
                parts(hidden_ps[:, s % HB, :], (w1h[:, e, rows], w1l[:, e, rows]),
                      (xfh[:, b.parity, cols], xfl[:, b.parity, cols]), True, True).then_inc(s_up, 1)

            def down(b, s):
                u, e, k = s // KT, s // KT % EXPERTS, s % KT
                if k == 0:
                    pe.wait_ge(s_weighted, b.index * UNITS + u - 1 + CREDIT)
                pe.wait_ge(s_lo, b.index * SLOTS + s + 1)
                last = parts(y_ps[:, u % 2, :], (w2h[:, e * KT + k, :], w2l[:, e * KT + k, :]),
                             (gh[:, s % HB, :], gl[:, s % HB, :]), k == 0, k == KT - 1)
                if k == KT - 1:
                    last.then_inc(s_down, 1)

            pe.wait_ge(s_wqkv, 6)
            pe.wait_ge(s_ident, 2)
            pe.wait_ge(s_const, POOL_CONSTS)
            for j in range(3):
                last = pe.transpose(ab[:, 0, j * P:(j + 1) * P], wqkv_raw[:, j, :], ident[:, :])
            last.then_inc(s_wtr, 1)
            pe.wait_ge(s_load_small, 16 * 7)
            n = EXPERTS * KT
            pe.transpose(ab[:, 1, 0:P], w_out_raw[:, :], ident[:, :])
            pe.transpose(ab[:, 1, P:P + n], b1_raw[:, :], ident[0:n, 0:n])
            pe.transpose(ab[:, 1, P + n:P + n + EXPERTS], b2_raw[:, :],
                         ident[0:EXPERTS, 0:EXPERTS]).then_inc(s_wtr, 1)
            pe.wait_ge(s_wready, WREADY)

            def body(b, a1, a2):
                def claim(name, known=()):
                    s, count = last_read_of(name, a1, a2)
                    if s not in known:
                        wait(pe, s, count)
                    return ab[:, BANK_OF[name], :]

                def turn(name, src, done):
                    bank = claim(name)
                    for k in range(HT):
                        last = pe.transpose(bank[:, k * P:(k + 1) * P], src(k), ident[:, :])
                    last.then_inc(done, 1)

                for s in range(SLOTS):
                    if a2 is not None:
                        n = a2.index
                        for h in [h for h in range(2) if s == PE_SLOT[f"F{h}"]]:
                            if h == 0:
                                pe.wait_ge(s_mix, n + 1)
                                pe.wait_ge(s_q_ch, n * 2 + 2)
                            bank = claim(f"F{h}", known=(s_mix, s_q_ch) if h == 0 else ())
                            for k in range(HT):
                                t = h * HT + k
                                last = pe.matmul(bank[:, k * P:(k + 1) * P], q_ch[:, a2.parity, t * P:(t + 1) * P],
                                                 mix[:, a2.parity, :], start=True, stop=True)
                            last.then_inc(s_fin, 1)
                        for h in [h for h in range(2) if s == PE_SLOT[f"O{h}"]]:
                            if h == 0:
                                pe.wait_ge(s_x1, n + 1)
                            turn(f"O{h}", lambda k: x1_tok[:, h * HT + k, :], s_o_tr)
                        for h in [h for h in range(2) if s == PE_SLOT[f"G{h}"]]:
                            if h == 0:
                                pe.wait_ge(s_xf, n + 1)
                            turn(f"G{h}", lambda k: xf_tok[:, h * HT + k, :], s_g_tr)
                        if s == PE_SLOT["L"]:
                            pe.wait_ge(s_xf_ch, n * 2 + 2)
                            bank = claim("L", known=(s_xf_ch,))
                            for t in range(TILES):
                                last = pe.matmul(bank[:, t * EXPERTS:(t + 1) * EXPERTS], xf_ch[:, t * P:(t + 1) * P],
                                                 gate_w_sb[:, :], start=True, stop=True)
                            last.then_inc(s_lg_mm, 1)
                        if s == PE_SLOT["W"]:
                            pe.wait_ge(s_gate, n * GATE + GATE)
                            pe.transpose(claim("W", known=(s_gate,))[:, 0:P],
                                         cw_tok[:, :, :, :].rearrange("p a e t -> p (a e t)"), ident[:, :]).then_inc(s_cw_mm, 1)
                    if a1 is not None:
                        n = a1.index
                        for h in [h for h in range(2) if s == PE_SLOT[f"X{h}"]]:
                            if h == 0:
                                pe.wait_ge(s_x_in[a1.parity], a1.pair * 16 + 16)
                            turn(f"X{h}", lambda k: x_sb[:, a1.parity, (h * HT + k) * P:(h * HT + k + 1) * P],
                                 s_x_tr)
                        for t in [t for t in range(TILES) if s == PE_SLOT[f"Q{t}"]]:
                            if t == 0:
                                pe.wait_ge(s_x_split, n * 2 + 2)
                            cols = slice(t * P, (t + 1) * P)
                            parts(claim(f"Q{t}")[:, 0:3 * P], (xh[:, cols], xl[:, cols]),
                                  (wqkv_h[:, :], wqkv_l[:, :]), True, True).then_inc(s_qkv_mm, 1)
                        if s == PE_SLOT["KT"]:
                            pe.wait_ge(s_k_part, n + 1)
                            pe.transpose(claim("KT")[:, 0:P], k_part[:, :], ident[:, :]).then_inc(s_kt_mm, 1)
                        if s == PE_SLOT["KB"]:
                            pe.wait_ge(s_k_max, n * 2 + 2)
                            pe.matmul(claim("KB")[:, 0:P], ones[:, :], k_diag[:, :], start=True,
                                      stop=True).then_inc(s_kb_mm, 1)
                        if s == PE_SLOT["C"]:
                            pe.wait_ge(s_exp, n * 2 + 2)
                            bank = claim("C")
                            for t in range(TILES):
                                pe.matmul(bank[:, 0:P], qkv[:, t, 2 * P:3 * P], qkv[:, t, P:2 * P],
                                          start=t == 0, stop=t == TILES - 1)
                            for t in range(TILES):
                                last = pe.matmul(bank[:, P:P + 2], qkv[:, t, P:2 * P], ones[:, 0:2],
                                                 start=t == 0, stop=t == TILES - 1)
                            last.then_inc(s_c_mm, 1)
                        if s == PE_SLOT["M"]:
                            pe.wait_ge(s_ctx, n * 2 + 1)
                            pe.matmul(claim("M")[:, 0:P], ctx_t[:, :], w_out_t[:, :], start=True,
                                      stop=True).then_inc(s_m_mm, 1)
                        for h in [h for h in range(2) if s == PE_SLOT[f"T{h}"]]:
                            if h == 0:
                                pe.wait_ge(s_q_norm, n + 1)
                            turn(f"T{h}", lambda k: qkv[:, h * HT + k, 0:P], s_q_tr)
                    if b is not None:
                        if s + AHEAD < SLOTS:
                            up(b, s + AHEAD)
                        elif a2 is not None:
                            up(a2, s + AHEAD - SLOTS)
                        down(b, s)
                if b is None and a2 is not None:
                    pe.wait_ge(s_wsplit, 4)
                    for s in range(AHEAD):
                        up(a2, s)

            run(pe, body)


_INS = ['x', 'L0_conv_W_qkv', 'L0_conv_W_out', 'L0_conv_b_out', 'L0_conv_g_norm', 'L0_conv_g_out',
        'L0_ffn_gate_w', 'L0_ffn_gate_b', 'L0_ffn_W1', 'L0_ffn_b1', 'L0_ffn_W2', 'L0_ffn_b2']
_OUTS = [((16, 128, 32, 32), 'float32')]


def kernel(**inputs):
    import numpy as _np
    import concourse.bacc as _bacc
    from concourse import mybir as _mybir
    from concourse.bass_utils import run_bass_kernel_spmd as _run

    nc = _bacc.Bacc("TRN2", target_bir_lowering=False, num_devices=1)
    arrays, args = {}, []
    for name in _INS:
        a = _np.ascontiguousarray(inputs[name])
        arrays[f"in_{name}_dram"] = a
        args.append(nc.dram_tensor(f"in_{name}_dram", a.shape, _mybir.dt.from_np(a.dtype), kind="ExternalInput").ap())
    for i, (shape, dtype) in enumerate(_OUTS):
        dt = _mybir.dt.from_np(_np.dtype(dtype))
        args.append(nc.dram_tensor(f"out_{i}_dram", shape, dt, kind="ExternalOutput").ap())
    build(nc, *args)
    r = _run(nc, [arrays], core_ids=[0])
    got = tuple(r.results[0][f"out_{i}_dram"] for i in range(len(_OUTS)))
    return got[0]
```

```python
from contextlib import ExitStack

import concourse.bass as bass
from concourse import mybir

ALU = mybir.AluOpType
ACT = mybir.ActivationFunctionType
X_AXIS = mybir.AxisListType.X
F32 = mybir.dt.float32
F32R = mybir.dt.float32r

P = 128
BATCH, CH, TOK = 16, 128, 1024
TILES = TOK // P
HALF = TOK // 2
HT = HALF // P
HEADS, HEAD_DIM = 4, 32
EXPERTS, HIDDEN = 8, 256
KT = HIDDEN // P
SLOTS = 2 * EXPERTS * KT
UNITS = 2 * EXPERTS
AHEAD = 4
LOW_AHEAD = 3
WB = 4
HB = 4
GB = 8
PICKS = 4
LOW_POOL = (0, 9, 11, 13, 23, 24, 26, 28)
LOW_VECTOR = tuple(s for s in range(SLOTS) if s not in LOW_POOL)
QKV_ACT = (1, 3, 5, 7)
QKV_VECTOR = tuple(t for t in range(TILES) if t not in QKV_ACT)
LN_C_EPS, LN_T_EPS, RMS_EPS = 1e-6, 1e-5, 1e-12

PE_SLOT = {"F0": 0.5, "F1": 0.5, "O0": 8, "X0": 9.5, "X1": 11, "O1": 11, "G0": 13, "G1": 13.5,
           "Q0": 15, "Q1": 16, "Q2": 16.5, "Q3": 16.5, "Q4": 17, "Q5": 17.5, "Q6": 17.5, "Q7": 18,
           "KT": 20, "L": 20.5, "KB": 21, "C": 24.5, "W": 26, "M": 28.5, "T0": 28.5, "T1": 30}
ACT_SLOT = {"square0": 0, "square1": 0, "x1_ch0": 8.5, "x_tok0": 9.5, "x_high": 10.5, "x_tok1": 10.5,
            "x1_ch1": 11.5, "xf_ch0": 12.5, "xf_ch1": 12.5, "qkv1": 15, "qkv3": 16, "qkv5": 17.5,
            "qkv7": 18, "exp": 21, "cw_rows": 26.5, "q_ch0": 29, "q_ch1": 29.5}
BANK_OF = {"F0": 0, "F1": 1, "X0": 1, "X1": 0, "O0": 0, "O1": 1, "G0": 0, "G1": 1, "Q0": 0, "Q1": 1, "Q2": 0,
           "Q3": 1, "Q4": 0, "Q5": 1, "Q6": 0, "Q7": 1, "L": 0, "KT": 1, "KB": 1, "W": 0, "C": 1, "M": 1,
           "T0": 0, "T1": 1}
DVE_SLOT = {"ss0": 0.5, "ss1": 0.5, "norm0": 2.5, "norm1": 2.5, "bn2_0": 7.5, "bn2_1": 8.5, "stats2": 9,
            "bn1_0": 9.5, "xf0": 10, "xf1": 10, "bn1_1": 10.5, "stats1": 13, "qkv0": 14.5, "qkv2": 15.5,
            "qkv4": 17, "qkv6": 17.5, "k_part": 18.5, "q_max": 19, "k_max": 19.5, "scores": 20,
            "k_shift": 21, "pick": 21.5, "q_sum": 22, "ctx": 26, "mix": 28.5}
SETUP_SLOT = {"high": 18, "small": 22, "w1_low": 22, "w2_low": 29}
POOL_SLOT = {"rms": 0, "x1": 4, "r2": 9, "x_low": 11, "r1": 13, "xf_low": 16, "q_shift": 20, "q_norm": 22,
             "k_fold": 22}
STAGE_1 = ("X0", "X1", "Q0", "Q1", "Q2", "Q3", "Q4", "Q5", "Q6", "Q7", "KT", "KB", "C", "M", "T0", "T1")
STAGE_2 = ("F0", "F1", "O0", "O1", "G0", "G1", "L", "W")
BANK_ORDER = sorted(STAGE_2 + STAGE_1, key=lambda name: PE_SLOT[name])


class Image:

    def __init__(self, pair, parity):
        self.pair, self.parity = pair, parity
        self.index = pair * 2 + parity

    def is_first(self):
        return isinstance(self.pair, int) and self.index == 0

    def plus(self, n):
        return Image(self.pair + (self.parity + n) // 2, (self.parity + n) % 2)


def wait(eng, sem, value):
    if not isinstance(value, int) or value > 0:
        eng.wait_ge(sem, value)


def build(nc, x, w_qkv, w_out, b_out, g_norm, g_out, gate_w, gate_b, w1, b1, w2, b2, out):
    x_dram = x.rearrange("b c h w -> (b c) (h w)")
    out_dram = out.rearrange("b c h w -> (b c) (h w)")
    w1_dram = w1.rearrange("e c h -> c e h")
    w2_dram = w2.rearrange("e (k p) d -> p (e k) d", p=P)
    scratch = nc.dram_tensor("routing_scratch", [2 * EXPERTS * TILES, P], F32, kind="Internal").ap()

    with ExitStack() as ctx:
        def sb(name, shape, dt=F32):
            return ctx.enter_context(nc.sbuf_tensor(name, shape, dt))

        def sem(name):
            return ctx.enter_context(nc.semaphore(name))

        hidden_ps = ctx.enter_context(nc.psum_tensor("hidden_ps", [P, HB, HALF], F32))
        y_ps = ctx.enter_context(nc.psum_tensor("y_ps", [P, 2, HALF], F32))
        ab = ctx.enter_context(nc.psum_tensor("ab", [P, 2, HALF], F32))

        ident = sb("ident", [P, P])
        ones = sb("ones", [P, P])
        head_mask = sb("head_mask", [P, P])
        minus_half = sb("minus_half", [P, TILES])
        rms_eps = sb("rms_eps", [P, TILES])
        rank = sb("rank", [P, EXPERTS])
        g_norm_bc = sb("g_norm_bc", [P, P])
        g_out_bc = sb("g_out_bc", [P, P])
        b_out_bc = sb("b_out_bc", [P, P])
        gate_b_bc = sb("gate_b_bc", [P, EXPERTS])
        gate_w_sb = sb("gate_w_sb", [P, EXPERTS])
        gate_w_parts = sb("gate_w_parts", [P, 2 * EXPERTS], F32R)
        w_mean = sb("w_mean", [P, 3])
        w_out_raw = sb("w_out_raw", [P, P])
        b1_raw = sb("b1_raw", [EXPERTS * KT, P])
        b2_raw = sb("b2_raw", [EXPERTS, P])
        wqkv_h = sb("wqkv_h", [P, 3 * P], F32R)
        wqkv_l = sb("wqkv_l", [P, 3 * P], F32R)
        w_out_t = sb("w_out_t", [P, P])
        b1_t = sb("b1_t", [P, EXPERTS * KT])
        b2_t = sb("b2_t", [P, EXPERTS])
        w1h = sb("w1h", [P, EXPERTS, HIDDEN], F32R)
        w1l = sb("w1l", [P, EXPERTS, HIDDEN], F32R)
        w2h = sb("w2h", [P, EXPERTS * KT, CH], F32R)
        w2l = sb("w2l", [P, EXPERTS * KT, CH], F32R)

        x_sb = sb("x_sb", [P, 2, TOK])
        xh = sb("xh", [P, TOK], F32R)
        xl = sb("xl", [P, TOK], F32R)
        x_tok = sb("x_tok", [P, 2, TILES, CH])
        bn1 = sb("bn1", [P, TILES, 6])
        st1 = sb("st1", [P, 5, TILES])
        r1 = sb("r1", [P, TILES])
        qkv = sb("qkv", [P, TILES, 3 * P])
        q_stat = sb("q_stat", [P, 3, TILES * HEADS])
        k_part = sb("k_part", [P, P])
        k_max = sb("k_max", [P, 1])
        k_diag = sb("k_diag", [P, P])
        ctx_t = sb("ctx_t", [P, P])
        k_fold = sb("k_fold", [P, TILES // 2, P])
        k_recip = sb("k_recip", [P, 1])
        mix = sb("mix", [P, 2, P])
        q_ch = sb("q_ch", [P, 2, TOK])

        square = sb("square", [P, 2, HALF])
        ss = sb("ss", [P, 2, TILES])
        r_rms = sb("r_rms", [P, TILES])
        x1_tok = sb("x1_tok", [P, TILES, CH])
        bn2 = sb("bn2", [P, TILES, 6])
        st2 = sb("st2", [P, 6, TILES])
        r2 = sb("r2", [P, TILES])
        xf_tok = sb("xf_tok", [P, TILES, CH])
        x1_ch = sb("x1_ch", [P, 2, TOK])
        xf_ch = sb("xf_ch", [P, TOK])
        xfh = sb("xfh", [P, 2, TOK], F32R)
        xfl = sb("xfl", [P, 2, TOK], F32R)
        gate = sb("gate", [P, 6, TILES, EXPERTS])
        gate_stat = sb("gate_stat", [P, 7, TILES])
        cw_tok = sb("cw_tok", [P, 2, EXPERTS, TILES])
        cw_rows = sb("cw_rows", [EXPERTS * TILES, P])
        cw = sb("cw", [P, 2, EXPERTS, HALF])

        gelu = sb("gelu", [P, HB, HALF])
        gh = sb("gh", [P, GB, HALF], F32R)
        gl = sb("gl", [P, HB, HALF], F32R)
        weighted = sb("weighted", [P, WB, HALF])

        wqkv_raw = cw[:, 0, 0, 0:3 * P].rearrange("p (j c) -> p j c", j=3)
        wqkv_c = cw[:, 0, 1, 0:3 * P].rearrange("p (j c) -> p j c", j=3)
        w1_raw = cw[:, 1, 0:4, :].rearrange("p a n -> p (a n)")
        w2_raw = cw[:, 1, 4:8, :].rearrange("p a n -> p (a n)")

        s_load_qkv, s_load_small, s_load_experts = sem("load_qkv"), sem("load_small"), sem("load_experts")
        s_const, s_ident = sem("const_done"), sem("ident_done")
        s_wqkv, s_wtr, s_wready = sem("wqkv_centered"), sem("weights_transposed"), sem("weights_ready")
        s_whigh, s_wsplit = sem("expert_weights_high"), sem("expert_weights_split")
        s_x_in = [sem("x_in0"), sem("x_in1")]
        s_x_split = sem("x_split")
        s_x_tr = sem("x_transposed")
        s_x_tok = sem("x_tok_done")
        s_st1 = sem("stats1_step")
        s_r1 = sem("r1_done")
        s_qkv_mm = sem("qkv_product")
        s_qkv, s_qkv_act = sem("qkv_scaled_vector"), sem("qkv_scaled_scalar")
        s_q_max, s_k_part = sem("q_max"), sem("k_part_max")
        s_q_sub, s_k_sub = sem("q_shifted"), sem("k_shifted")
        s_kt_mm, s_k_max, s_kb_mm = sem("k_max_transposed"), sem("k_max_step"), sem("k_max_spread")
        s_exp = sem("exp_done")
        s_k_fold = sem("k_folded")
        s_q_sum, s_q_norm = sem("q_sum_step"), sem("q_normalised")
        s_c_mm, s_ctx, s_m_mm = sem("context"), sem("context_done"), sem("mix_product")
        s_k_sum_mm, s_k_recip, s_mix = sem("k_sum"), sem("k_reciprocal"), sem("mix_done")
        s_q_tr, s_q_ch = sem("q_transposed"), sem("q_ch_done")
        s_fin, s_square, s_ss = sem("attention_out"), sem("square_done"), sem("square_sum")
        s_rms, s_y, s_x1 = sem("rms_step"), sem("normed_out"), sem("x1_done")
        s_st2, s_r2, s_xf = sem("stats2_step"), sem("r2_done"), sem("xf_done")
        s_o_tr, s_x1_ch = sem("x1_transposed"), sem("x1_ch_done")
        s_g_tr, s_xf_ch = sem("xf_transposed"), sem("xf_ch_done")
        s_xf_split = sem("xf_split")
        s_lg_mm, s_gate, s_gate_exp = sem("logits"), sem("gate_step"), sem("gate_exp")
        s_cw_mm, s_cw_rows, s_scratch = sem("cw_transposed"), sem("cw_rows_done"), sem("cw_in_dram")
        s_cw_in = [[sem(f"cw_in{h}{q}") for q in range(2)] for h in range(2)]
        s_up, s_gelu, s_down = sem("up_done"), sem("gelu_done"), sem("down_done")
        s_lo, s_lo_pool = sem("low_done_vector"), sem("low_done_gpsimd")
        s_weighted, s_added = sem("weighted_done"), sem("added_done")
        s_out = [[sem(f"stored{p}{h}") for h in range(2)] for p in range(2)]

        ST1, ST2, GATE = 5, 7, 20
        WREADY = 7
        POOL_CONSTS = 3 + EXPERTS
        CREDIT, STORE_CREDIT = 4, 16

        READ_OUT = {"F0": (s_y, 2, 1), "F1": (s_y, 2, 2), "X0": (s_x_tok, 2, 1), "X1": (s_x_tok, 2, 2),
                    "O0": (s_x1_ch, 2, 1), "O1": (s_x1_ch, 2, 2), "G0": (s_xf_ch, 2, 1), "G1": (s_xf_ch, 2, 2),
                    "L": (s_gate, GATE, 2), "KT": (s_k_max, 2, 1), "KB": (s_k_sub, 1, 1), "W": (s_cw_rows, 1, 1),
                    "C": (s_ctx, 1, 1), "T0": (s_q_ch, 2, 1), "M": (s_mix, 1, 1), "T1": (s_q_ch, 2, 2)}
        for sem_qkv, tiles in ((s_qkv, QKV_VECTOR), (s_qkv_act, QKV_ACT)):
            READ_OUT.update({f"Q{t}": (sem_qkv, len(tiles), k + 1) for k, t in enumerate(tiles)})

        def wait_low(eng, b, s):
            if s < 0:
                b, s = b.plus(-1), s + SLOTS
            sem_lo, slots = (s_lo_pool, LOW_POOL) if s in LOW_POOL else (s_lo, LOW_VECTOR)
            wait(eng, sem_lo, b.index * len(slots) + slots.index(s) + 1)

        def low_part(eng, b, s):
            eng.wait_ge(s_gelu, b.index * SLOTS + s + 1)
            eng.wait_ge(s_down, b.index * SLOTS + s + 1 - HB + CREDIT)
            eng.tensor_tensor(gl[:, s % HB, :], gelu[:, s % HB, :], gh[:, s % GB, :].bitcast(F32),
                              ALU.subtract).then_inc(s_lo_pool if s in LOW_POOL else s_lo, 1)

        def last_read_of(name, a1, a2):
            def stage(n):
                return 2 if n in STAGE_2 else 1

            order = [n for n in BANK_ORDER if BANK_OF[n] == BANK_OF[name]]
            image = {1: None if a1 is None else a1.index, 2: None if a2 is None else a2.index}
            before = {1: (BATCH if a1 is None else a1.index) - 1, 2: -1 if a2 is None else a2.index - 1}
            for n in reversed(order[:order.index(name)]):
                if image[stage(n)] is not None:
                    s, per, k = READ_OUT[n]
                    return s, image[stage(n)] * per + k
            for n in reversed(order):
                index = before[stage(n)]
                if not isinstance(index, int) or index >= 0:
                    s, per, k = READ_OUT[n]
                    return s, index * per + k
            return None, 0

        def run(eng, body):
            body(None, Image(0, 0), None)
            body(None, Image(0, 1), Image(0, 0))
            with eng.Fori(0, BATCH // 2 - 1) as pair:
                for parity in range(2):
                    b = Image(pair, parity)
                    body(b, b.plus(2), b.plus(1))
            body(Image(BATCH // 2 - 1, 0), None, Image(BATCH // 2 - 1, 1))
            body(Image(BATCH // 2 - 1, 1), None, None)

        block = ctx.enter_context(nc.Block())

        @block.sync
        def _(sp):
            def load_x(a):
                wait(sp, s_x_split, (a.index - 1) * 2)
                wait(sp, s_x_tr, (a.index - 1) * 2)
                sp.dma_start(x_sb[:, a.parity, :], x_dram[bass.ds(a.index * P, P), :]).then_inc(s_x_in[a.parity], 16)

            sp.dma_start(wqkv_raw, w_qkv.rearrange("(j o) c -> o j c", j=3)).then_inc(s_load_qkv, 16)
            sp.dma_start(g_norm_bc[:, :], g_norm.partition_broadcast(P)).then_inc(s_load_qkv, 16)
            load_x(Image(0, 0))
            sp.dma_start(w1_raw.rearrange("p (e h) -> p e h", e=EXPERTS), w1_dram).then_inc(s_load_experts, 16)
            sp.dma_start(w2_raw.rearrange("p (e d) -> p e d", d=CH), w2_dram).then_inc(s_load_experts, 16)

            def body(b, a1, a2):
                if a1 is not None and not (b is None and a2 is None):
                    load_x(a1)
                if b is not None:
                    store(b, 0)
                if a2 is not None:
                    rows = EXPERTS * TILES
                    wait(sp, s_cw_rows, a2.index + 1)
                    image_rows = scratch[a2.parity * rows:(a2.parity + 1) * rows, :]
                    sp.dma_start(image_rows, cw_rows[:, :]).then_inc(s_scratch, 16)
                    sp.wait_ge(s_scratch, (a2.index + 1) * 16)
                    for h in range(2):
                        if b is not None:
                            sp.wait_ge(s_weighted, b.index * UNITS + (h + 1) * EXPERTS + CREDIT)
                        elif h == 1:
                            sp.wait_ge(s_wsplit, 2)
                        for q in range(2):
                            half_rows = image_rows.rearrange(
                                "(e t) n -> e t n", e=EXPERTS)[q * 4:q * 4 + 4, h * HT:(h + 1) * HT, :]
                            sp.dma_start(cw[:, h, q * 4:q * 4 + 4, :],
                                         half_rows.rearrange("e t n -> e (t n)").partition_broadcast(P)
                                         ).then_inc(s_cw_in[h][q], 16)
                if b is not None:
                    store(b, 1)

            def store(b, h):
                sp.wait_ge(s_added, b.index * UNITS + (h + 1) * EXPERTS + CREDIT)
                sp.dma_start(out_dram[bass.ds(b.index * P, P), h * HALF:(h + 1) * HALF],
                             x1_ch[:, b.parity, h * HALF:(h + 1) * HALF]).then_inc(s_out[b.parity][h], 16)

            run(sp, body)
            for p in range(2):
                for h in range(2):
                    sp.wait_ge(s_out[p][h], 16 * (BATCH // 2) + STORE_CREDIT)

        @block.gpsimd
        def _(pool):
            pool.memset(ident[:, :], 0.0).then_inc(s_ident, 1)
            pool.memset(ones[:, :], 1.0).then_inc(s_const, 1)
            pool.memset(minus_half[:, :], -0.5).then_inc(s_const, 1)
            pool.memset(rms_eps[:, :], RMS_EPS).then_inc(s_const, 1)
            pool.memset(weighted[:, 0, 0:1], 0.0).then_inc(s_added, CREDIT)
            for p in range(2):
                for h in range(2):
                    pool.memset(weighted[:, 1, 2 * p + h:2 * p + h + 1], 0.0).then_inc(s_out[p][h], STORE_CREDIT)
            for e in range(EXPERTS):
                pool.memset(rank[:, e:e + 1], float(EXPERTS - e)).then_inc(s_const, 1)
            pool.wait_ge(s_ident, 1)
            pool.affine_select(out=ident[:, :], in_=ident[:, :], compare_op=ALU.not_equal, fill=1.0,
                               base=0, pattern=[[-1, P]], channel_multiplier=1).then_inc(s_ident, 1)
            pool.wait_ge(s_const, POOL_CONSTS)

            def add(b, s):
                u = s // KT
                h = u // EXPERTS
                dst = x1_ch[:, b.parity, h * HALF:(h + 1) * HALF]
                if u % EXPERTS == 0:
                    pool.wait_ge(s_x1_ch, b.index * 2 + h + 1)
                else:
                    pool.wait_ge(s_added, b.index * UNITS + u + CREDIT)
                pool.wait_ge(s_weighted, b.index * UNITS + u + 1 + CREDIT)
                pool.tensor_tensor(dst, dst, weighted[:, u % WB, :], ALU.add).then_inc(s_added, 1)

            def x_low(a):
                pool.wait_ge(s_x_split, a.index * 2 + 1)
                pool.tensor_tensor(xl[:, :], x_sb[:, a.parity, :], xh[:, :].bitcast(F32),
                                   ALU.subtract).then_inc(s_x_split, 1)

            def body(b, a1, a2):
                for s in range(SLOTS):
                    if a2 is not None:
                        n = a2.index
                        if s == POOL_SLOT["rms"]:
                            wait(pool, s_y, n * 2)
                            pool.wait_ge(s_ss, n * 2 + 2)
                            pool.tensor_tensor(ss[:, 1, :], ss[:, 0, :], rms_eps[:, :], ALU.add).then_inc(s_rms, 1)
                            pool.wait_ge(s_rms, n * 2 + 1)
                            pool.tensor_tensor(r_rms[:, :], ss[:, 1, :], minus_half[:, :], ALU.pow).then_inc(s_rms, 1)
                        if s == POOL_SLOT["x1"]:
                            pool.wait_ge(s_y, n * 2 + 2)
                            pool.tensor_tensor(x1_tok[:, :, :], x_tok[:, a2.parity, :, :], x1_tok[:, :, :],
                                               ALU.add).then_inc(s_x1, 1)
                        if s == POOL_SLOT["r2"]:
                            pool.wait_ge(s_st2, n * ST2 + ST2)
                            pool.tensor_tensor(r2[:, :], st2[:, 3, :], minus_half[:, :], ALU.pow).then_inc(s_r2, 1)
                        if s == POOL_SLOT["xf_low"]:
                            pool.wait_ge(s_xf_ch, n * 2 + 2)
                            pool.tensor_tensor(xfl[:, a2.parity, :], xf_ch[:, :],
                                               xfh[:, a2.parity, :].bitcast(F32), ALU.subtract).then_inc(s_xf_split, 1)
                    if a1 is not None:
                        n = a1.index
                        if s == POOL_SLOT["x_low"] and not (b is None and a2 is not None):
                            x_low(a1)
                        if s == POOL_SLOT["r1"]:
                            wait(pool, s_qkv, n * len(QKV_VECTOR))
                            wait(pool, s_qkv_act, n * len(QKV_ACT))
                            pool.wait_ge(s_st1, n * ST1 + ST1)
                            pool.tensor_tensor(r1[:, :], st1[:, 4, :], minus_half[:, :], ALU.pow).then_inc(s_r1, 1)
                        if s == POOL_SLOT["q_shift"]:
                            pool.wait_ge(s_q_max, n + 1)
                            q = qkv[:, :, 0:P].rearrange("p t (h d) -> p t h d", d=HEAD_DIM)
                            m = q_stat[:, 0, :].rearrange("p (t h) -> p t h", h=HEADS).unsqueeze(3).broadcast_to(
                                (P, TILES, HEADS, HEAD_DIM))
                            pool.tensor_tensor(q, q, m, ALU.subtract).then_inc(s_q_sub, 1)
                        if s == POOL_SLOT["k_fold"]:
                            pool.wait_ge(s_exp, n * 2 + 2)
                            wait(pool, s_k_sum_mm, n)
                            pool.tensor_tensor(k_fold[:, 0:4, :], qkv[:, 0:4, P:2 * P], qkv[:, 4:8, P:2 * P],
                                               ALU.add).then_inc(s_k_fold, 1)
                            pool.wait_ge(s_k_fold, n * 3 + 1)
                            pool.tensor_tensor(k_fold[:, 0:2, :], k_fold[:, 0:2, :], k_fold[:, 2:4, :],
                                               ALU.add).then_inc(s_k_fold, 1)
                            pool.wait_ge(s_k_fold, n * 3 + 2)
                            pool.tensor_tensor(k_fold[:, 0, :], k_fold[:, 0, :], k_fold[:, 1, :],
                                               ALU.add).then_inc(s_k_fold, 1)
                        if s == POOL_SLOT["q_norm"]:
                            pool.wait_ge(s_q_sum, n * 2 + 2)
                            q = qkv[:, :, 0:P].rearrange("p t (h d) -> p t h d", d=HEAD_DIM)
                            m = q_stat[:, 2, :].rearrange("p (t h) -> p t h", h=HEADS).unsqueeze(3).broadcast_to(
                                (P, TILES, HEADS, HEAD_DIM))
                            pool.tensor_tensor(q, q, m, ALU.mult).then_inc(s_q_norm, 1)
                    ahead = s + LOW_AHEAD
                    if ahead >= SLOTS:
                        if a2 is not None and ahead - SLOTS in LOW_POOL:
                            low_part(pool, a2, ahead - SLOTS)
                    elif b is not None and ahead in LOW_POOL:
                        low_part(pool, b, ahead)
                    if b is not None and s % KT == 1 and s > 1:
                        add(b, s - KT)
                if b is not None:
                    add(b, SLOTS - 1)
                if b is None and a2 is None:
                    x_low(a1.plus(1))

            run(pool, body)

        @block.scalar
        def _(act):
            act.dma_start(w_out_raw[:, :], w_out).then_inc(s_load_small, 16)
            act.dma_start(b1_raw[:, :], b1.rearrange("e (k p) -> (e k) p", p=P)).then_inc(s_load_small, 16)
            act.dma_start(b2_raw[:, :], b2).then_inc(s_load_small, 16)
            act.dma_start(g_out_bc[:, :], g_out.partition_broadcast(P)).then_inc(s_load_small, 16)
            act.dma_start(b_out_bc[:, :], b_out.partition_broadcast(P)).then_inc(s_load_small, 16)
            act.dma_start(gate_b_bc[:, :], gate_b.partition_broadcast(P)).then_inc(s_load_small, 16)
            act.dma_start(gate_w_sb[:, :], gate_w).then_inc(s_load_small, 16)

            def gelu_high(b, s):
                if s == 0 and b.is_first():
                    act.wait_ge(s_wready, WREADY)
                act.wait_ge(s_up, b.index * SLOTS + s + 1)
                act.activation(gh[:, s % GB, :], hidden_ps[:, s % HB, :], ACT.Gelu,
                               bias=b1_t[:, s % UNITS:s % UNITS + 1])

            def gelu_full(b, s):
                wait_low(act, b, s - HB)
                act.activation(gelu[:, s % HB, :], hidden_ps[:, s % HB, :], ACT.Gelu,
                               bias=b1_t[:, s % UNITS:s % UNITS + 1]).then_inc(s_gelu, 1)

            def x_high(a):
                act.wait_ge(s_x_in[a.parity], a.pair * 16 + 16)
                wait(act, s_qkv_mm, a.index * TILES)
                act.activation(xh[:, :], x_sb[:, a.parity, :], ACT.Copy).then_inc(s_x_split, 1)

            def body(b, a1, a2):
                for slot in range(SLOTS):
                    def of_slot(part):
                        if slot + AHEAD >= SLOTS:
                            if a2 is not None:
                                part(a2, slot + AHEAD - SLOTS)
                        elif b is not None:
                            part(b, slot + AHEAD)

                    steps(slot, b, a1, a2)
                    of_slot(gelu_high)
                    steps(slot + 0.5, b, a1, a2)
                    of_slot(gelu_full)
                    if b is None and a2 is None and slot == SETUP_SLOT["high"]:
                        act.wait_ge(s_load_experts, 32)
                        for high, raw in ((w1h, w1_raw), (w2h, w2_raw)):
                            act.activation(high[:, :, :].rearrange("p e n -> p (e n)"), raw,
                                           ACT.Copy).then_inc(s_whigh, 1)
                if b is None and a2 is None:
                    x_high(a1.plus(1))

            def steps(s, b, a1, a2):
                if a2 is not None:
                    n = a2.index
                    for h in [h for h in range(2) if s == ACT_SLOT[f"square{h}"]]:
                        act.wait_ge(s_fin, n * 2 + h + 1)
                        act.activation(square[:, h, :], ab[:, BANK_OF[f"F{h}"], :], ACT.Square).then_inc(s_square, 1)
                    for h in [h for h in range(2) if s == ACT_SLOT[f"x1_ch{h}"]]:
                        if h == 0:
                            for k in range(2):
                                act.wait_ge(s_out[a2.parity][k], a2.pair * 16 + STORE_CREDIT)
                        act.wait_ge(s_o_tr, n * 2 + h + 1)
                        act.activation(x1_ch[:, a2.parity, h * HALF:(h + 1) * HALF],
                                       ab[:, BANK_OF[f"O{h}"], :], ACT.Copy).then_inc(s_x1_ch, 1)
                    for h in [h for h in range(2) if s == ACT_SLOT[f"xf_ch{h}"]]:
                        act.wait_ge(s_g_tr, n * 2 + h + 1)
                        if h == 0:
                            wait(act, s_xf_split, n)
                            if b is not None:
                                act.wait_ge(s_up, b.index * SLOTS + AHEAD)
                        cols, bank = slice(h * HALF, (h + 1) * HALF), ab[:, BANK_OF[f"G{h}"], :]
                        act.activation(xf_ch[:, cols], bank, ACT.Copy)
                        act.activation(xfh[:, a2.parity, cols], bank, ACT.Copy).then_inc(s_xf_ch, 1)
                    if s == ACT_SLOT["exp"]:
                        act.wait_ge(s_gate, n * GATE + 4)
                        act.activation(gate[:, 1, :, :], gate[:, 0, :, :], ACT.Exp).then_inc(s_gate_exp, 1)
                    if s == ACT_SLOT["cw_rows"]:
                        wait(act, s_scratch, n * 16)
                        act.wait_ge(s_cw_mm, n + 1)
                        act.activation(cw_rows[:, :], ab[0:EXPERTS * TILES, BANK_OF["W"], 0:P],
                                       ACT.Copy).then_inc(s_cw_rows, 1)
                if a1 is not None:
                    n = a1.index
                    if s == ACT_SLOT["x_high"] and not (b is None and a2 is not None):
                        x_high(a1)
                    for h in [h for h in range(2) if s == ACT_SLOT[f"x_tok{h}"]]:
                        if h == 0:
                            wait(act, s_x1, n - 1)
                        act.wait_ge(s_x_tr, n * 2 + h + 1)
                        act.activation(x_tok[:, a1.parity, h * HT:(h + 1) * HT, :].rearrange("p t c -> p (t c)"),
                                       ab[:, BANK_OF[f"X{h}"], :], ACT.Copy).then_inc(s_x_tok, 1)
                    for t in [t for t in QKV_ACT if s == ACT_SLOT[f"qkv{t}"]]:
                        if t == QKV_ACT[0]:
                            act.wait_ge(s_r1, n + 1)
                            wait(act, s_c_mm, n)
                            wait(act, s_q_tr, n * 2)
                        act.wait_ge(s_qkv_mm, n * TILES + t + 1)
                        act.activation(qkv[:, t, :], ab[:, BANK_OF[f"Q{t}"], 0:3 * P], ACT.Copy,
                                       scale=r1[:, t:t + 1]).then_inc(s_qkv_act, 1)
                    if s == ACT_SLOT["exp"]:
                        for sem_sub, j in ((s_q_sub, 0), (s_k_sub, 1)):
                            act.wait_ge(sem_sub, n + 1)
                            part = qkv[:, :, j * P:(j + 1) * P]
                            act.activation(part, part, ACT.Exp).then_inc(s_exp, 1)
                    for h in [h for h in range(2) if s == ACT_SLOT[f"q_ch{h}"]]:
                        act.wait_ge(s_q_tr, n * 2 + h + 1)
                        if h == 0:
                            wait(act, s_fin, (n - 1) * 2)
                        act.activation(q_ch[:, a1.parity, h * HALF:(h + 1) * HALF], ab[:, BANK_OF[f"T{h}"], :],
                                       ACT.Copy).then_inc(s_q_ch, 1)

            run(act, body)

        @block.vector
        def _(dve):
            for i in range(HEADS):
                rows = slice(i * HEAD_DIM, (i + 1) * HEAD_DIM)
                for j in range(HEADS):
                    dve.memset(head_mask[rows, j * HEAD_DIM:(j + 1) * HEAD_DIM],
                               float(HEAD_DIM) ** -0.5 if i == j else 0.0)
            dve.memset(cw_tok[:, 1, :, :], 0.0)
            dve.memset(w_mean[:, 0:1], 0.0).then_inc(s_weighted, CREDIT)
            dve.memset(w_mean[:, 1:2], 0.0).then_inc(s_down, CREDIT)
            dve.wait_ge(s_weighted, CREDIT)
            dve.wait_ge(s_down, CREDIT)
            dve.wait_ge(s_const, POOL_CONSTS)
            dve.wait_ge(s_ident, 2)
            dve.wait_ge(s_load_qkv, 32)
            dve.tensor_tensor(wqkv_c, wqkv_raw, g_norm_bc[:, :].unsqueeze(1).broadcast_to((P, 3, P)),
                              ALU.mult).then_inc(s_wqkv, 1)
            dve.wait_ge(s_wqkv, 1)
            dve.tensor_reduce(w_mean[:, :], wqkv_c, X_AXIS, ALU.add).then_inc(s_wqkv, 1)
            dve.wait_ge(s_wqkv, 2)
            dve.tensor_scalar(w_mean[:, :], w_mean[:, :], 1.0 / CH, None, ALU.mult).then_inc(s_wqkv, 1)
            dve.wait_ge(s_wqkv, 3)
            for j in range(3):
                dve.tensor_scalar(wqkv_raw[:, j, :], wqkv_c[:, j, :], w_mean[:, j:j + 1], None,
                                  ALU.subtract).then_inc(s_wqkv, 1)
            dve.wait_ge(s_wtr, 1)
            dve.tensor_copy(wqkv_h[:, :], hidden_ps[:, 0, 0:3 * P]).then_inc(s_wqkv, 1)
            dve.wait_ge(s_wqkv, 7)
            dve.tensor_tensor(wqkv_l[:, :], hidden_ps[:, 0, 0:3 * P], wqkv_h[:, :].bitcast(F32),
                              ALU.subtract).then_inc(s_wqkv, 1)

            def prepare_small():
                dve.wait_ge(s_load_small, 16 * 7)
                dve.tensor_scalar(g_out_bc[:, :], g_out_bc[:, :], float(CH) ** 0.5, None,
                                  ALU.mult).then_inc(s_wready, 1)
                dve.tensor_scalar(b_out_bc[:, :], b_out_bc[:, :], 1.0 / HEADS, None, ALU.mult).then_inc(s_wready, 1)
                dve.tensor_copy(gate_w_parts[:, 0:EXPERTS], gate_w_sb[:, :]).then_inc(s_wready, 1)
                dve.wait_ge(s_wready, 3)
                dve.tensor_tensor(gate_w_parts[:, EXPERTS:2 * EXPERTS], gate_w_sb[:, :],
                                  gate_w_parts[:, 0:EXPERTS].bitcast(F32), ALU.subtract).then_inc(s_wready, 1)
                dve.wait_ge(s_wtr, 2)
                n = EXPERTS * KT
                dve.tensor_copy(w_out_t[:, :], hidden_ps[:, 1, 0:P]).then_inc(s_wready, 1)
                dve.tensor_copy(b1_t[:, :], hidden_ps[:, 1, P:P + n]).then_inc(s_wready, 1)
                dve.tensor_copy(b2_t[:, :], hidden_ps[:, 1, P + n:P + n + EXPERTS]).then_inc(s_wready, 1)
                dve.wait_ge(s_wready, WREADY)

            def expert_lows(high, low, raw, k):
                dve.wait_ge(s_whigh, k)
                high, low = (w[:, :, :].rearrange("p e n -> p (e n)") for w in (high, low))
                dve.tensor_tensor(low, raw, high.bitcast(F32), ALU.subtract).then_inc(s_wsplit, 1)

            def low(b, s):
                if s in LOW_VECTOR:
                    low_part(dve, b, s)

            def weigh(b, s):
                u = s // KT
                h, e = u // EXPERTS, u % EXPERTS
                if e % 4 == 0:
                    dve.wait_ge(s_cw_in[h][e // 4], b.index * 16 + 16)
                dve.wait_ge(s_added, b.index * UNITS + u + 1 - WB + CREDIT)
                dve.wait_ge(s_down, b.index * SLOTS + s + 1 + CREDIT)
                dve.scalar_tensor_tensor(out=weighted[:, u % WB, :], in0=y_ps[:, u % 2, :], scalar=b2_t[:, e:e + 1],
                                         in1=cw[:, h, e, :], op0=ALU.add, op1=ALU.mult).then_inc(s_weighted, 1)

            def body(b, a1, a2):
                for slot in range(SLOTS):
                    steps(slot, a1, a2)
                    if b is None and a2 is None:
                        if slot == SETUP_SLOT["small"]:
                            prepare_small()
                        if slot == SETUP_SLOT["w1_low"]:
                            expert_lows(w1h, w1l, w1_raw, 1)
                        if slot == SETUP_SLOT["w2_low"]:
                            expert_lows(w2h, w2l, w2_raw, 2)
                    if slot + LOW_AHEAD >= SLOTS:
                        if a2 is not None:
                            low(a2, slot + LOW_AHEAD - SLOTS)
                    elif b is not None:
                        low(b, slot + LOW_AHEAD)
                    steps(slot + 0.5, a1, a2)
                    if b is not None and slot % KT == KT - 1:
                        weigh(b, slot)

            def steps(s, a1, a2):
                if a2 is not None:
                    n = a2.index
                    for h in [h for h in range(2) if s == DVE_SLOT[f"ss{h}"]]:
                        if h == 0:
                            wait(dve, s_rms, n * 2)
                        dve.wait_ge(s_square, n * 2 + h + 1)
                        dve.tensor_reduce(ss[:, 0, h * HT:(h + 1) * HT],
                                          square[:, h, :].rearrange("p (t c) -> p t c", c=CH),
                                          X_AXIS, ALU.add).then_inc(s_ss, 1)
                    for h in [h for h in range(2) if s == DVE_SLOT[f"norm{h}"]]:
                        dve.wait_ge(s_rms, n * 2 + 2)
                        if h == 0:
                            wait(dve, s_o_tr, n * 2)
                            wait(dve, s_xf, n * 2)
                        bank = ab[:, BANK_OF[f"F{h}"], :]
                        for k in range(HT):
                            t = h * HT + k
                            last = dve.scalar_tensor_tensor(
                                out=x1_tok[:, t, :], in0=bank[:, k * P:(k + 1) * P], scalar=r_rms[:, t:t + 1],
                                in1=g_out_bc[:, :], op0=ALU.mult, op1=ALU.mult)
                        last.then_inc(s_y, 1)
                    for h in [h for h in range(2) if s == DVE_SLOT[f"bn2_{h}"]]:
                        dve.wait_ge(s_x1, n + 1)
                        if h == 0:
                            wait(dve, s_r2, n)
                        for t in range(h * HT, (h + 1) * HT):
                            last = dve.bn_stats(bn2[:, t, :], x1_tok[:, t, :])
                        if h == 1:
                            last.then_inc(s_st2, 1)
                    if s == DVE_SLOT["stats2"]:
                        dve.wait_ge(s_st2, n * ST2 + 1)
                        stats2(n * ST2)
                    for h in [h for h in range(2) if s == DVE_SLOT[f"xf{h}"]]:
                        if h == 0:
                            dve.wait_ge(s_r2, n + 1)
                            wait(dve, s_g_tr, n * 2)
                        for t in range(h * HT, (h + 1) * HT):
                            last = dve.tensor_scalar(xf_tok[:, t, :], x1_tok[:, t, :], st2[:, 5, t:t + 1],
                                                     r2[:, t:t + 1], ALU.subtract, ALU.mult)
                        last.then_inc(s_xf, 1)
                    if s == DVE_SLOT["scores"]:
                        gate_scores(n)
                    first = 5 + int((s - DVE_SLOT["pick"]) * 2) * PICKS
                    for k in range(max(first, 5), min(first + PICKS, GATE + 1)):
                        gate_pick(n, k)
                if a1 is not None:
                    attention(s, a1)

            def stats2(base):
                def then(ins, k):
                    ins.then_inc(s_st2, 1)
                    dve.wait_ge(s_st2, base + k)
                mean_e, m2_e, mean_o, m2_o = (bn2[:, :, k] for k in (1, 2, 4, 5))
                then(dve.tensor_tensor(st2[:, 0, :], mean_e, mean_o, ALU.subtract), 2)
                then(dve.tensor_tensor(st2[:, 4, :], mean_e, mean_o, ALU.add), 3)
                then(dve.tensor_tensor(st2[:, 1, :], m2_e, m2_o, ALU.add), 4)
                dve.tensor_scalar(st2[:, 5, :], st2[:, 4, :], 0.5, None, ALU.mult)
                dve.tensor_scalar(st2[:, 1, :], st2[:, 1, :], 1.0 / CH, LN_T_EPS, ALU.mult, ALU.add).then_inc(s_st2, 1)
                then(dve.scalar_tensor_tensor(out=st2[:, 2, :], in0=st2[:, 0, :], scalar=0.25, in1=st2[:, 0, :],
                                              op0=ALU.mult, op1=ALU.mult), 6)
                dve.tensor_tensor(st2[:, 3, :], st2[:, 1, :], st2[:, 2, :], ALU.add).then_inc(s_st2, 1)

            def stats1(base):
                def then(ins, k):
                    ins.then_inc(s_st1, 1)
                    dve.wait_ge(s_st1, base + k)
                mean_e, m2_e, mean_o, m2_o = (bn1[:, :, k] for k in (1, 2, 4, 5))
                dve.tensor_tensor(st1[:, 0, :], mean_e, mean_o, ALU.subtract)
                then(dve.tensor_tensor(st1[:, 1, :], m2_e, m2_o, ALU.add), 2)
                dve.tensor_scalar(st1[:, 3, :], st1[:, 1, :], 1.0 / CH, RMS_EPS * LN_C_EPS / CH, ALU.mult, ALU.add)
                then(dve.scalar_tensor_tensor(out=st1[:, 2, :], in0=st1[:, 0, :], scalar=0.25, in1=st1[:, 0, :],
                                              op0=ALU.mult, op1=ALU.mult), 3)
                then(dve.tensor_tensor(st1[:, 2, :], st1[:, 2, :], st1[:, 3, :], ALU.add), 4)
                dve.tensor_scalar(st1[:, 4, :], st1[:, 2, :], 1.0 + RMS_EPS / CH, None, ALU.mult).then_inc(s_st1, 1)

            def over_experts(k):
                return gate_stat[:, k, :].unsqueeze(2).broadcast_to((P, TILES, EXPERTS))

            def gate_scores(n):
                logits = ab[:, BANK_OF["L"], 0:TILES * 2 * EXPERTS].rearrange("p (t e) -> p t e", e=2 * EXPERTS)
                dve.wait_ge(s_lg_mm, n + 1)
                dve.tensor_tensor(gate[:, 0, :, :], logits[:, :, 0:EXPERTS], gate_b_bc[:, :].unsqueeze(1).broadcast_to(
                    (P, TILES, EXPERTS)), ALU.add).then_inc(s_gate, 1)
                dve.wait_ge(s_gate, n * GATE + 1)
                dve.tensor_tensor(gate[:, 2, :, :], gate[:, 0, :, :], logits[:, :, EXPERTS:2 * EXPERTS],
                                  ALU.add).then_inc(s_gate, 1)
                dve.wait_ge(s_gate, n * GATE + 2)
                dve.tensor_reduce(gate_stat[:, 0, :], gate[:, 2, :, :], X_AXIS, ALU.max).then_inc(s_gate, 1)
                dve.wait_ge(s_gate, n * GATE + 3)
                dve.tensor_tensor(gate[:, 0, :, :], gate[:, 2, :, :], over_experts(0), ALU.subtract).then_inc(s_gate, 1)

            def gate_pick(n, k):
                ranks = rank[:, :].unsqueeze(1).broadcast_to((P, TILES, EXPERTS))
                exps, probs, first, rest, second = (gate[:, i, :, :] for i in range(1, 6))

                def maximum(j, src):
                    return dve.tensor_reduce(gate_stat[:, j, :], src, X_AXIS, ALU.max)

                if k == 5:
                    dve.wait_ge(s_gate_exp, n + 1)
                    step = dve.tensor_reduce(gate_stat[:, 1, :], exps, X_AXIS, ALU.add)
                else:
                    dve.wait_ge(s_gate, n * GATE + k - 1)
                if k == 6:
                    step = dve.reciprocal(gate_stat[:, 2, :], gate_stat[:, 1, :])
                if k == 7:
                    step = dve.tensor_tensor(probs, exps, over_experts(2), ALU.mult)
                if k == 8:
                    step = maximum(3, probs)
                if k == 9:
                    step = dve.tensor_tensor(first, probs, over_experts(3), ALU.is_equal)
                if k == 10:
                    step = dve.tensor_tensor(first, first, ranks, ALU.mult)
                if k == 11:
                    step = maximum(4, first)
                if k == 12:
                    step = dve.tensor_tensor(first, first, over_experts(4), ALU.is_equal)
                if k == 13:
                    step = dve.scalar_tensor_tensor(out=rest, in0=first, scalar=-2.0, in1=probs, op0=ALU.mult,
                                                    op1=ALU.add)
                if k == 14:
                    step = maximum(5, rest)
                if k == 15:
                    step = dve.tensor_tensor(second, rest, over_experts(5), ALU.is_equal)
                if k == 16:
                    step = dve.tensor_tensor(second, second, ranks, ALU.mult)
                if k == 17:
                    step = maximum(6, second)
                if k == 18:
                    step = dve.tensor_tensor(second, second, over_experts(6), ALU.is_equal)
                if k == 19:
                    step = dve.tensor_tensor(first, first, second, ALU.add)
                if k == 20:
                    wait(dve, s_cw_mm, n)
                    step = dve.tensor_tensor(cw_tok[:, 0, :, :].rearrange("p e t -> p t e"), first, probs, ALU.mult)
                step.then_inc(s_gate, 1)

            def attention(s, a1):
                n = a1.index
                for h in [h for h in range(2) if s == DVE_SLOT[f"bn1_{h}"]]:
                    dve.wait_ge(s_x_tok, n * 2 + h + 1)
                    if h == 0:
                        wait(dve, s_r1, n)
                    for t in range(h * HT, (h + 1) * HT):
                        last = dve.bn_stats(bn1[:, t, :], x_tok[:, a1.parity, t, :])
                    if h == 1:
                        last.then_inc(s_st1, 1)
                if s == DVE_SLOT["stats1"]:
                    dve.wait_ge(s_st1, n * ST1 + 1)
                    stats1(n * ST1)
                for t in [t for t in QKV_VECTOR if s == DVE_SLOT[f"qkv{t}"]]:
                    if t == QKV_VECTOR[0]:
                        dve.wait_ge(s_r1, n + 1)
                        wait(dve, s_c_mm, n)
                        wait(dve, s_q_tr, n * 2)
                    dve.wait_ge(s_qkv_mm, n * TILES + t + 1)
                    dve.tensor_scalar(qkv[:, t, :], ab[:, BANK_OF[f"Q{t}"], 0:3 * P], r1[:, t:t + 1], None,
                                      ALU.mult).then_inc(s_qkv, 1)
                if s == DVE_SLOT["q_max"]:
                    dve.wait_ge(s_qkv, (n + 1) * len(QKV_VECTOR))
                    dve.wait_ge(s_qkv_act, (n + 1) * len(QKV_ACT))
                    dve.tensor_reduce(q_stat[:, 0, :].rearrange("p (t h) -> p t h", h=HEADS),
                                      qkv[:, :, 0:P].rearrange("p t (h d) -> p t h d", d=HEAD_DIM),
                                      X_AXIS, ALU.max).then_inc(s_q_max, 1)
                if s == DVE_SLOT["k_part"]:
                    dve.wait_ge(s_qkv, (n + 1) * len(QKV_VECTOR))
                    dve.wait_ge(s_qkv_act, (n + 1) * len(QKV_ACT))
                    wait(dve, s_kt_mm, n)
                    dve.tensor_reduce(k_part[:, :], qkv[:, :, P:2 * P].rearrange("p t c -> p c t"),
                                      X_AXIS, ALU.max).then_inc(s_k_part, 1)
                if s == DVE_SLOT["k_max"]:
                    dve.wait_ge(s_kt_mm, n + 1)
                    dve.tensor_reduce(k_max[:, :], ab[:, BANK_OF["KT"], 0:P], X_AXIS, ALU.max).then_inc(s_k_max, 1)
                    dve.wait_ge(s_k_max, n * 2 + 1)
                    dve.tensor_scalar(k_diag[:, :], ident[:, :], k_max[:, 0:1], None, ALU.mult).then_inc(s_k_max, 1)
                if s == DVE_SLOT["k_shift"]:
                    dve.wait_ge(s_kb_mm, n + 1)
                    k = qkv[:, :, P:2 * P]
                    dve.tensor_tensor(k, k, ab[:, BANK_OF["KB"], 0:P].unsqueeze(1).broadcast_to((P, TILES, P)),
                                      ALU.subtract).then_inc(s_k_sub, 1)
                if s == DVE_SLOT["q_sum"]:
                    dve.wait_ge(s_exp, n * 2 + 1)
                    dve.tensor_reduce(q_stat[:, 1, :].rearrange("p (t h) -> p t h", h=HEADS),
                                      qkv[:, :, 0:P].rearrange("p t (h d) -> p t h d", d=HEAD_DIM),
                                      X_AXIS, ALU.add).then_inc(s_q_sum, 1)
                    dve.wait_ge(s_q_sum, n * 2 + 1)
                    dve.reciprocal(q_stat[:, 2, :], q_stat[:, 1, :]).then_inc(s_q_sum, 1)
                if s == DVE_SLOT["ctx"]:
                    dve.wait_ge(s_c_mm, n + 1)
                    wait(dve, s_m_mm, n)
                    wait(dve, s_mix, n)
                    dve.tensor_tensor(ctx_t[:, :], ab[:, BANK_OF["C"], 0:P], head_mask[:, :],
                                      ALU.mult).then_inc(s_ctx, 1)
                if s == DVE_SLOT["mix"]:
                    dve.wait_ge(s_m_mm, n + 1)
                    dve.wait_ge(s_k_sum_mm, n + 1)
                    dve.reciprocal(k_recip[:, :], ab[:, BANK_OF["M"], P:P + 1]).then_inc(s_k_recip, 1)
                    dve.wait_ge(s_k_recip, n + 1)
                    wait(dve, s_fin, (n - 1) * 2)
                    dve.scalar_tensor_tensor(out=mix[:, a1.parity, :], in0=ab[:, BANK_OF["M"], 0:P],
                                             scalar=k_recip[:, 0:1], in1=b_out_bc[:, :], op0=ALU.mult,
                                             op1=ALU.add).then_inc(s_mix, 1)

            run(dve, body)

        @block.tensor
        def _(pe):
            def parts(out_ap, lhs, rhs, start, stop):
                (lh, ll), (rh, rl) = lhs, rhs
                pe.matmul(out_ap, lh, rh, start=start, stop=False)
                pe.matmul(out_ap, ll, rh, start=False, stop=False)
                return pe.matmul(out_ap, lh, rl, start=False, stop=stop)

            def up(b, s):
                e, k, h = s // KT % EXPERTS, s % KT, s // UNITS
                if s == 0:
                    pe.wait_ge(s_xf_split, b.index + 1)
                if s == 0 and b.is_first():
                    pe.wait_ge(s_wsplit, 2)
                    pe.wait_ge(s_wready, WREADY)
                wait(pe, s_gelu, b.index * SLOTS + s + 1 - HB)
                cols = slice(h * HALF, (h + 1) * HALF)
                rows = slice(k * P, (k + 1) * P)
                parts(hidden_ps[:, s % HB, :], (w1h[:, e, rows], w1l[:, e, rows]),
                      (xfh[:, b.parity, cols], xfl[:, b.parity, cols]), True, True).then_inc(s_up, 1)

            def down(b, s):
                u, e, k = s // KT, s // KT % EXPERTS, s % KT
                if k == 0:
                    pe.wait_ge(s_weighted, b.index * UNITS + u - 1 + CREDIT)
                wait_low(pe, b, s)
                last = parts(y_ps[:, u % 2, :], (w2h[:, e * KT + k, :], w2l[:, e * KT + k, :]),
                             (gh[:, s % GB, :], gl[:, s % HB, :]), k == 0, k == KT - 1)
                last.then_inc(s_down, 1)

            pe.wait_ge(s_wqkv, 6)
            pe.wait_ge(s_ident, 2)
            pe.wait_ge(s_const, POOL_CONSTS)
            for j in range(3):
                last = pe.transpose(hidden_ps[:, 0, j * P:(j + 1) * P], wqkv_raw[:, j, :], ident[:, :])
            last.then_inc(s_wtr, 1)

            def transpose_small():
                n = EXPERTS * KT
                pe.wait_ge(s_load_small, 16 * 7)
                pe.transpose(hidden_ps[:, 1, 0:P], w_out_raw[:, :], ident[:, :])
                pe.transpose(hidden_ps[:, 1, P:P + n], b1_raw[:, :], ident[0:n, 0:n])
                pe.transpose(hidden_ps[:, 1, P + n:P + n + EXPERTS], b2_raw[:, :],
                             ident[0:EXPERTS, 0:EXPERTS]).then_inc(s_wtr, 1)

            def body(b, a1, a2):
                def claim(name, known=()):
                    s, count = last_read_of(name, a1, a2)
                    if s is not None and s not in known:
                        wait(pe, s, count)
                    return ab[:, BANK_OF[name], :]

                def turn(name, src, done):
                    bank = claim(name)
                    for k in range(HT):
                        last = pe.transpose(bank[:, k * P:(k + 1) * P], src(k), ident[:, :])
                    last.then_inc(done, 1)

                def steps(s):
                    if a2 is not None:
                        n = a2.index
                        for h in [h for h in range(2) if s == PE_SLOT[f"F{h}"]]:
                            if h == 0:
                                pe.wait_ge(s_mix, n + 1)
                                pe.wait_ge(s_q_ch, n * 2 + 2)
                            bank = claim(f"F{h}", known=(s_mix, s_q_ch) if h == 0 else ())
                            for k in range(HT):
                                t = h * HT + k
                                last = pe.matmul(bank[:, k * P:(k + 1) * P], q_ch[:, a2.parity, t * P:(t + 1) * P],
                                                 mix[:, a2.parity, :], start=True, stop=True)
                            last.then_inc(s_fin, 1)
                        for h in [h for h in range(2) if s == PE_SLOT[f"O{h}"]]:
                            if h == 0:
                                pe.wait_ge(s_x1, n + 1)
                            turn(f"O{h}", lambda k: x1_tok[:, h * HT + k, :], s_o_tr)
                        for h in [h for h in range(2) if s == PE_SLOT[f"G{h}"]]:
                            pe.wait_ge(s_xf, n * 2 + h + 1)
                            turn(f"G{h}", lambda k: xf_tok[:, h * HT + k, :], s_g_tr)
                        if s == PE_SLOT["L"]:
                            pe.wait_ge(s_xf_split, n + 1)
                            bank = claim("L")
                            for t in range(TILES):
                                cols, logits = slice(t * P, (t + 1) * P), bank[:, t * 2 * EXPERTS:(t + 1) * 2 * EXPERTS]
                                pe.matmul(logits, xfh[:, a2.parity, cols], gate_w_parts[:, :], start=True, stop=False)
                                last = pe.matmul(logits, xfl[:, a2.parity, cols], gate_w_parts[:, :], start=False,
                                                 stop=True)
                            last.then_inc(s_lg_mm, 1)
                        if s == PE_SLOT["W"]:
                            pe.wait_ge(s_gate, n * GATE + GATE)
                            weights = cw_tok[:, :, :, :].rearrange("p a e t -> p (a e t)")
                            pe.transpose(claim("W", known=(s_gate,))[:, 0:P], weights, ident[:, :]).then_inc(s_cw_mm, 1)
                    if a1 is not None:
                        n = a1.index
                        for h in [h for h in range(2) if s == PE_SLOT[f"X{h}"]]:
                            if h == 0:
                                pe.wait_ge(s_x_in[a1.parity], a1.pair * 16 + 16)
                            turn(f"X{h}", lambda k: x_sb[:, a1.parity, (h * HT + k) * P:(h * HT + k + 1) * P],
                                 s_x_tr)
                        for t in [t for t in range(TILES) if s == PE_SLOT[f"Q{t}"]]:
                            if t == 0:
                                pe.wait_ge(s_wqkv, 8)
                                pe.wait_ge(s_x_split, n * 2 + 2)
                            cols = slice(t * P, (t + 1) * P)
                            parts(claim(f"Q{t}")[:, 0:3 * P], (xh[:, cols], xl[:, cols]),
                                  (wqkv_h[:, :], wqkv_l[:, :]), True, True).then_inc(s_qkv_mm, 1)
                        if s == PE_SLOT["KT"]:
                            pe.wait_ge(s_k_part, n + 1)
                            pe.transpose(claim("KT")[:, 0:P], k_part[:, :], ident[:, :]).then_inc(s_kt_mm, 1)
                        if s == PE_SLOT["KB"]:
                            pe.wait_ge(s_k_max, n * 2 + 2)
                            pe.matmul(claim("KB")[:, 0:P], ones[:, :], k_diag[:, :], start=True,
                                      stop=True).then_inc(s_kb_mm, 1)
                        if s == PE_SLOT["C"]:
                            pe.wait_ge(s_exp, n * 2 + 2)
                            bank = claim("C")
                            for t in range(TILES):
                                last = pe.matmul(bank[:, 0:P], qkv[:, t, 2 * P:3 * P], qkv[:, t, P:2 * P],
                                                 start=t == 0, stop=t == TILES - 1)
                            last.then_inc(s_c_mm, 1)
                        if s == PE_SLOT["M"]:
                            pe.wait_ge(s_ctx, n + 1)
                            pe.wait_ge(s_wready, WREADY)
                            bank = claim("M")
                            pe.matmul(bank[:, 0:P], ctx_t[:, :], w_out_t[:, :], start=True,
                                      stop=True).then_inc(s_m_mm, 1)
                            pe.wait_ge(s_k_fold, n * 3 + 3)
                            pe.matmul(bank[:, P:P + 2], k_fold[:, 0, :], ones[:, 0:2], start=True,
                                      stop=True).then_inc(s_k_sum_mm, 1)
                        for h in [h for h in range(2) if s == PE_SLOT[f"T{h}"]]:
                            if h == 0:
                                pe.wait_ge(s_q_norm, n + 1)
                            turn(f"T{h}", lambda k: qkv[:, h * HT + k, 0:P], s_q_tr)

                for slot in range(SLOTS):
                    steps(slot)
                    if b is None and a2 is None and slot == SETUP_SLOT["small"]:
                        transpose_small()
                    if slot + AHEAD >= SLOTS:
                        if a2 is not None:
                            up(a2, slot + AHEAD - SLOTS)
                    elif b is not None:
                        up(b, slot + AHEAD)
                    steps(slot + 0.5)
                    if b is not None:
                        down(b, slot)

            run(pe, body)


_INS = ['x', 'L0_conv_W_qkv', 'L0_conv_W_out', 'L0_conv_b_out', 'L0_conv_g_norm', 'L0_conv_g_out',
        'L0_ffn_gate_w', 'L0_ffn_gate_b', 'L0_ffn_W1', 'L0_ffn_b1', 'L0_ffn_W2', 'L0_ffn_b2']
_OUTS = [((16, 128, 32, 32), 'float32')]


def kernel(**inputs):
    import numpy as _np
    import concourse.bacc as _bacc
    from concourse import mybir as _mybir
    from concourse.bass_utils import run_bass_kernel_spmd as _run

    nc = _bacc.Bacc("TRN2", target_bir_lowering=False, num_devices=1)
    arrays, args = {}, []
    for name in _INS:
        a = _np.ascontiguousarray(inputs[name])
        arrays[f"in_{name}_dram"] = a
        args.append(nc.dram_tensor(f"in_{name}_dram", a.shape, _mybir.dt.from_np(a.dtype), kind="ExternalInput").ap())
    for i, (shape, dtype) in enumerate(_OUTS):
        dt = _mybir.dt.from_np(_np.dtype(dtype))
        args.append(nc.dram_tensor(f"out_{i}_dram", shape, dt, kind="ExternalOutput").ap())
    build(nc, *args)
    r = _run(nc, [arrays], core_ids=[0])
    got = tuple(r.results[0][f"out_{i}_dram"] for i in range(len(_OUTS)))
    return got[0]
```
